# Optimizing a Trainium2 kernel written in Bass

```python
import numpy as np
import jax
import jax.numpy as jnp

def _softmax(x, axis=-1):
    return jax.nn.softmax(x, axis=axis)

def _gelu(x):
    return jax.nn.gelu(x, approximate=True)

def _silu(x):
    return jax.nn.silu(x)

def _sigmoid(x):
    return jax.nn.sigmoid(x)

def _layernorm(x, axis=-1, eps=1e-05):
    m = jnp.mean(x, axis=axis, keepdims=True)
    v = jnp.var(x, axis=axis, keepdims=True)
    return (x - m) / jnp.sqrt(v + eps)

def _scatter_add(tgt, idx, src, axis=0):
    return tgt.at[idx].add(src)

def _segment_sum(src, seg, n):
    return jax.ops.segment_sum(src, seg, n)
kernel_name = 'mk_sandwich_d1_jaxref_r8_9dc564'

def setup_inputs(seed: int=0):
    np.random.seed(seed)
    _w = jnp.asarray

    def _L0_attn_setup():
        import jax, jax.numpy as jnp
        import numpy as np
        D_MODEL = 128
        NHEAD = 16
        D_K = D_MODEL // NHEAD
        MAX_REL = 128
        key = jax.random.key(seed)
        ks = jax.random.split(key, 6)
        B, S = (4, 256)
        s = 1.0 / np.sqrt(D_MODEL)
        x = jax.random.normal(ks[0], (B, S, D_MODEL), dtype=jnp.float32)
        W_qkv = jax.random.normal(ks[1], (D_MODEL, 3 * D_MODEL), dtype=jnp.float32) * s
        b_qkv = jnp.zeros((3 * D_MODEL,), dtype=jnp.float32)
        W_out = jax.random.normal(ks[2], (D_MODEL, D_MODEL), dtype=jnp.float32) * s
        b_out = jnp.zeros((D_MODEL,), dtype=jnp.float32)
        rel_bias = jax.random.normal(ks[3], (2 * MAX_REL + 1, NHEAD), dtype=jnp.float32) * 0.02
        return {'x': x, 'W_qkv': W_qkv, 'b_qkv': b_qkv, 'W_out': W_out, 'b_out': b_out, 'rel_bias': rel_bias}
    _L0_attn_in = _L0_attn_setup()

    def _L0_ffn_setup():
        import jax, jax.numpy as jnp
        import numpy as np
        D_IN, D_HID = (128, 512)

        def _ternary(key, shape):
            return jax.random.randint(key, shape, -1, 2).astype(jnp.float32)

        def _tlin(x, w, s):
            return jnp.einsum('bsi,oi->bso', x, w) * s
        key = jax.random.key(seed)
        ks = jax.random.split(key, 12)
        inv = lambda fan: 1.0 / np.sqrt(fan).astype(np.float32)
        return {'x': jax.random.normal(ks[0], (4, 256, D_IN), dtype=jnp.float32), 'w1_w': _ternary(ks[1], (D_HID, D_IN)), 'w1_s': jax.random.uniform(ks[2], (D_HID,), dtype=jnp.float32) * inv(D_IN), 'w2_w': _ternary(ks[3], (D_HID, D_IN)), 'w2_s': jax.random.uniform(ks[4], (D_HID,), dtype=jnp.float32) * inv(D_IN), 'h1_w': _ternary(ks[5], (D_HID, D_HID)), 'h1_s': jax.random.uniform(ks[6], (D_HID,), dtype=jnp.float32) * inv(D_HID), 'h2_w': _ternary(ks[7], (D_HID, D_HID)), 'h2_s': jax.random.uniform(ks[8], (D_HID,), dtype=jnp.float32) * inv(D_HID), 'w3_w': _ternary(ks[9], (D_IN, D_HID)), 'w3_s': jax.random.uniform(ks[10], (D_IN,), dtype=jnp.float32) * inv(D_HID)}
    _L0_ffn_in = _L0_ffn_setup()
    _d = {'L0_attn_x': _L0_attn_in['x'], 'L0_attn_W_qkv': _L0_attn_in['W_qkv'], 'L0_attn_b_qkv': _L0_attn_in['b_qkv'], 'L0_attn_W_out': _L0_attn_in['W_out'], 'L0_attn_b_out': _L0_attn_in['b_out'], 'L0_attn_rel_bias': _L0_attn_in['rel_bias'], 'L0_ffn_w1_w': _L0_ffn_in['w1_w'], 'L0_ffn_w1_s': _L0_ffn_in['w1_s'], 'L0_ffn_w2_w': _L0_ffn_in['w2_w'], 'L0_ffn_w2_s': _L0_ffn_in['w2_s'], 'L0_ffn_h1_w': _L0_ffn_in['h1_w'], 'L0_ffn_h1_s': _L0_ffn_in['h1_s'], 'L0_ffn_h2_w': _L0_ffn_in['h2_w'], 'L0_ffn_h2_s': _L0_ffn_in['h2_s'], 'L0_ffn_w3_w': _L0_ffn_in['w3_w'], 'L0_ffn_w3_s': _L0_ffn_in['w3_s']}
    _x0 = _d['L0_attn_x']
    _d['L0_attn_x'] = jax.random.normal(jax.random.fold_in(jax.random.key(seed), 1), (8, 256, 128), dtype=_x0.dtype)
    del _x0
    return _d

def reference(L0_attn_x, L0_attn_W_qkv, L0_attn_b_qkv, L0_attn_W_out, L0_attn_b_out, L0_attn_rel_bias, L0_ffn_w1_w, L0_ffn_w1_s, L0_ffn_w2_w, L0_ffn_w2_s, L0_ffn_h1_w, L0_ffn_h1_s, L0_ffn_h2_w, L0_ffn_h2_s, L0_ffn_w3_w, L0_ffn_w3_s):

    def _L0_attn_ref(x, W_qkv, b_qkv, W_out, b_out, rel_bias):
        import jax, jax.numpy as jnp
        import numpy as np
        D_MODEL = 128
        NHEAD = 16
        D_K = D_MODEL // NHEAD
        MAX_REL = 128
        B, S, D = x.shape
        qkv = x @ W_qkv + b_qkv
        qkv = qkv.reshape(B, S, 3, NHEAD, D_K)
        q, k, v = (qkv[:, :, 0], qkv[:, :, 1], qkv[:, :, 2])
        scores = jnp.einsum('bihd,bjhd->bhij', q, k) / jnp.sqrt(jnp.float32(D_K))
        idxs = jnp.arange(S)
        rel = jnp.clip(idxs[:, None] - idxs[None, :] + MAX_REL, 0, 2 * MAX_REL)
        bias = rel_bias[rel]
        scores = scores + jnp.transpose(bias, (2, 0, 1))[None]
        attn = jax.nn.softmax(scores, axis=-1)
        out = jnp.einsum('bhij,bjhd->bihd', attn, v).reshape(B, S, D)
        return out @ W_out + b_out

    def _L0_ffn_ref(x, w1_w, w1_s, w2_w, w2_s, h1_w, h1_s, h2_w, h2_s, w3_w, w3_s):
        import jax, jax.numpy as jnp
        import numpy as np
        D_IN, D_HID = (128, 512)

        def _ternary(key, shape):
            return jax.random.randint(key, shape, -1, 2).astype(jnp.float32)

        def _tlin(x, w, s):
            return jnp.einsum('bsi,oi->bso', x, w) * s
        h = jax.nn.silu(_tlin(x, w1_w, w1_s)) * _tlin(x, w2_w, w2_s)
        h = jax.nn.gelu(_tlin(h, h1_w, h1_s), approximate=False)
        h = jax.nn.gelu(_tlin(h, h2_w, h2_s), approximate=False)
        return _tlin(h, w3_w, w3_s)
    x = L0_attn_x
    x = x + _layernorm(_L0_attn_ref(_layernorm(x, axis=-1), L0_attn_W_qkv, L0_attn_b_qkv, L0_attn_W_out, L0_attn_b_out, L0_attn_rel_bias), axis=-1)
    x = x + _layernorm(_L0_ffn_ref(_layernorm(x, axis=-1), L0_ffn_w1_w, L0_ffn_w1_s, L0_ffn_w2_w, L0_ffn_w2_s, L0_ffn_h1_w, L0_ffn_h1_s, L0_ffn_h2_w, L0_ffn_h2_s, L0_ffn_w3_w, L0_ffn_w3_s), axis=-1)
    return x

_drawn_inputs = setup_inputs


def setup_inputs(seed=0):
    import zlib

    import numpy as np

    out = dict(_drawn_inputs(seed))
    spreads = {'L0_attn_b_qkv': (0.0, 0.1), 'L0_attn_b_out': (0.0, 0.1)}
    factors = {'L0_attn_rel_bias': 7.081}
    for name, (base, spread) in spreads.items():
        noise = np.random.default_rng([zlib.crc32(name.encode()), seed]).standard_normal(out[name].shape)
        drawn = base * np.exp(spread * noise) if base else spread * noise
        out[name] = jnp.asarray(drawn.astype(out[name].dtype))
    for name, factor in factors.items():
        out[name] = (out[name] * factor).astype(out[name].dtype)
    return out
```

```python
import concourse.bass as bass
from concourse import mybir
from contextlib import ExitStack

F32 = mybir.dt.float32
F32R = mybir.dt.float32r
ALU = mybir.AluOpType
ACT = mybir.ActivationFunctionType

B, S, D = 8, 256, 128
H, DK = 16, 8
HID = 512
P = 128
EPS = 1e-5
TOK = B * S
NT = TOK // P
TPB = S // P
MAX_REL = 128
REL = 2 * MAX_REL + 1
WIN = P + S
EXT = WIN + P - 1
CH = 512
NCH = TOK // CH
TPC = CH // P
NK = HID // P
PAIRS = H // 2
GROUPS = H // 4
HALF = H // 2
PARTS = 4
KROWS = PARTS * DK
VC = DK + 1
PADS = 128
PRING = 4


def windows(ap, start, step, count, width):
    return bass.AP(tensor=ap.tensor, offset=ap.offset + start, ap=[list(ap.ap[0]), [step, count], [1, width]])


def reverse(ap):
    n = ap.shape[-1]
    return bass.AP(tensor=ap.tensor, offset=ap.offset + n - 1, ap=[list(ap.ap[0]), [-1, n]])


def reverse_rows(ap):
    (row, m), (_, n) = ap.ap[1], ap.ap[2]
    return bass.AP(tensor=ap.tensor, offset=ap.offset + n - 1, ap=[list(ap.ap[0]), [row, m], [-1, n]])


def build(nc, x, wq, wk, wv, bq, bk, bv, wo, bo, ext, ext_max, w1, s1, w2, s2, h1, h1s, h2, h2s, w3, w3s,
          ident_in, out):
    ctx = ExitStack()
    with ctx:
        def sb(name, shape, dt=F32):
            return ctx.enter_context(nc.sbuf_tensor(name, shape, dt))

        def sem(name):
            return ctx.enter_context(nc.semaphore(name))

        ident = sb("ident", [P, P])
        identr = sb("identr", [P, P], F32R)
        wq_sb = sb("wq_sb", [P, D])
        wk_sb = sb("wk_sb", [P, D])
        wv_sb = sb("wv_sb", [P, D])
        wo_sb = sb("wo_sb", [P, D])
        bq_sb = sb("bq_sb", [P, 2])
        bv_bc = sb("bv_bc", [P, D])
        bo_bc = sb("bo_bc", [P, D])
        w3s_bc = sb("w3s_bc", [P, D])
        xs = sb("xs", [P, NT, D])
        stats = sb("stats", [P, TPC, 6])
        mv = sb("mv", [P, TPC, 2])
        rstd = sb("rstd", [P, TPC])
        mhalf = sb("mhalf", [P, TPC])
        xn = sb("xn", [P, TPC, D])
        xT = sb("xT", [P, CH])
        qk_hi = sb("qk_hi", [P, 2, CH], F32R)
        qk_lo = sb("qk_lo", [P, 2, CH], F32R)
        q_rows = sb("q_rows", [P, 2, HALF, S], F32R)
        k_rows = sb("k_rows", [P, 2, HALF, S], F32R)
        vx = sb("vx", [P, NT, H, VC])
        v_near = sb("v_near", [P, 2, TPB, H, VC])
        big = sb("big", [P, NK * TOK])
        bias_max = big[:, 0:H * WIN].rearrange("p (h c) -> p h c", h=H)
        bias_hi = sb("bias_hi", [P, H, WIN], F32R)
        bias_lo = sb("bias_lo", [P, H, WIN], F32R)
        pad = sb("pad", [P, PADS])
        mx = sb("mx", [P, TPB, H])
        mrow = sb("mrow", [HALF, 2, S], F32R)
        ring = sb("ring", [P, PRING * 4 * S])
        probs = ring[:, :].rearrange("p (a k j n) -> p a k j n", a=PRING, k=2, j=2)
        bias_raw = ring[:, 0:2 * 4 * WIN].rearrange("p (a h c) -> p a h c", a=2, h=4)
        oT = big[:, H * WIN:H * WIN + 2 * GROUPS * S].rearrange(
            "p (a g n) -> p a g n", a=2, g=GROUPS)
        qk_f = big[:, H * WIN:H * WIN + 2 * CH].rearrange("p (a n) -> p a n", a=2)
        rsum = sb("rsum", [P, H])
        on = sb("on", [P, TPB, D])
        onT = sb("onT", [P, S])
        y = sb("y", [P, TPB, D])
        z = sb("z", [P, TPB, D])
        zT = sb("zT", [P, TOK])
        w1_sb = sb("w1_sb", [P, HID])
        w2_sb = sb("w2_sb", [P, HID])
        h1_sb = sb("h1_sb", [P, NK, HID])
        h2_sb = sb("h2_sb", [P, NK, HID])
        w3_sb = sb("w3_sb", [P, NK, D])
        hs = sb("hs", [P, 4, NK])
        g0 = big[:, :].rearrange("p (k n) -> p k n", k=NK)
        a1 = ring[:, 0:NK * CH].rearrange("p (k n) -> p k n", k=NK)
        a2 = ring[:, NK * CH:2 * NK * CH].rearrange("p (k n) -> p k n", k=NK)
        gate = sb("gate", [P, 2, CH])

        st = [ctx.enter_context(nc.psum_tensor(f"st{i}", [P, 2, 2 * S], F32)) for i in range(2)]
        ms = [ctx.enter_context(nc.psum_tensor(f"ms{i}", [P, 2, S], F32)) for i in range(2)]
        pv = ctx.enter_context(nc.psum_tensor("pv", [P, 512], F32))
        misc = ctx.enter_context(nc.psum_tensor("misc", [P, 512], F32))
        bank = [st[0][:, 0, :], st[0][:, 1, :], st[1][:, 0, :], st[1][:, 1, :],
                ms[0][:, :, :].rearrange("p a n -> p (a n)"), ms[1][:, :, :].rearrange("p a n -> p (a n)"),
                pv[:, :], misc[:, :]]

        HBANK = ((0, 1, 2, 3), (4, 5, 6, 3))

        q_dram = nc.dram_tensor("q_parts", (2, P, TOK), F32, kind="Internal").ap()
        k_dram = nc.dram_tensor("k_parts", (2, P, TOK), F32, kind="Internal").ap()

        x_in = sem("x_in")
        qkv_w_in = sem("qkv_w_in")
        max_bias_in = sem("max_bias_in")
        raw_in = [sem(f"raw_in{i}") for i in range(2)]
        ffn_w_in = sem("ffn_w_in")
        const_set = sem("const_set")
        psum_zeroed = sem("psum_zeroed")
        identr_set = sem("identr_set")
        bias_hi_set = sem("bias_hi_set")
        bias_lo_set = sem("bias_lo_set")
        dve_order = sem("dve_order")
        var_set = sem("var_set")
        rstd_set = sem("rstd_set")
        xn_set = sem("xn_set")
        xnT_ready = sem("xnT_ready")
        xT_set = sem("xT_set")
        q_ready = sem("q_ready")
        k_ready = sem("k_ready")
        v_ready = sem("v_ready")
        qk_f_set = sem("qk_f_set")
        qk_hi_set = sem("qk_hi_set")
        qk_lo_set = sem("qk_lo_set")
        v_set = sem("v_set")
        parts_out = sem("parts_out")
        rows_in = [[sem(f"rows_in{i}{p}") for p in range(2)] for i in range(2)]
        mrow_in = [sem(f"mrow_in{i}") for i in range(2)]
        ms_ready = sem("ms_ready")
        ms_read = sem("ms_read")
        mT_ready = sem("mT_ready")
        mrow_set = sem("mrow_set")
        st_ready = sem("st_ready")
        exp_done = sem("exp_done")
        pv_ready = sem("pv_ready")
        oT_set = sem("oT_set")
        o_ready = sem("o_ready")
        on_set = sem("on_set")
        onT_ready = sem("onT_ready")
        onT_set = sem("onT_set")
        y_ready = sem("y_ready")
        y_read = sem("y_read")
        y_norm = sem("y_norm")
        x1_set = sem("x1_set")
        v_near_set = sem("v_near_set")
        z_set = sem("z_set")
        zT_ready = sem("zT_ready")
        zT_set = sem("zT_set")
        up_ready = sem("up_ready")
        silu_done = sem("silu_done")
        g0_set = sem("g0_set")
        a1_ready = sem("a1_ready")
        a1_set = sem("a1_set")
        a2_ready = sem("a2_ready")
        a2_set = sem("a2_set")
        y3_ready = sem("y3_ready")
        y3_read = sem("y3_read")
        y3_norm = sem("y3_norm")
        out_set = sem("out_set")
        out_done = sem("out_done")

        block = ctx.enter_context(nc.Block())

        ROW_DMAS = 2 * PARTS
        PARTS_OUT = 4 * 16

        def loop_batches(eng, batch):
            batch(0, 0)
            with eng.Fori(0, (B - 2) // 2) as i:
                batch(i * 2 + 1, 1)
                batch(i * 2 + 2, 0)
            batch(B - 1, 1)

        @block.sync
        def _(sp):
            xv = x.rearrange("(t p) d -> p t d", p=P)
            for c in range(NCH):
                sp.dma_start(xs[:, c * TPC:(c + 1) * TPC, :], xv[:, c * TPC:(c + 1) * TPC, :]).then_inc(x_in, 16)
                if c == 0:
                    for dst, src in ((ident, ident_in), (wq_sb, wq), (wk_sb, wk), (wv_sb, wv), (bq_sb[:, 0:1], bq),
                                     (bq_sb[:, 1:2], bk), (bv_bc, bv.broadcast_to((P, D))),
                                     (wo_sb, wo), (bo_bc, bo.broadcast_to((P, D))),
                                     (w3s_bc, w3s.broadcast_to((P, D)))):
                        sp.dma_start(dst[:, :], src).then_inc(qkv_w_in, 16)
            sp.dma_start(bias_max[:, :, :], bass.AP(tensor=ext_max.tensor, offset=0,
                                                    ap=[[1, P], [EXT, H], [1, WIN]])).then_inc(max_bias_in, 16)
            for g in range(4):
                if g >= 2:
                    sp.wait_ge(bias_hi_set, g - 1)
                    sp.wait_ge(bias_lo_set, g - 1)
                sp.dma_start(bias_raw[:, g % 2, :, :],
                             bass.AP(tensor=ext.tensor, offset=4 * g * EXT,
                                     ap=[[1, P], [EXT, 4], [1, WIN]])).then_inc(raw_in[g % 2], 16)
                if g == 1:
                    with sp.Fori(0, NCH) as c:
                        tok = bass.ds(c * CH, CH)
                        sp.wait_ge(qk_hi_set, c * 2 + 2)
                        sp.dma_start(q_dram[0, :, tok], qk_hi[:, 0, :].bitcast(F32)).then_inc(parts_out, 16)
                        sp.dma_start(k_dram[0, :, tok], qk_hi[:, 1, :].bitcast(F32)).then_inc(parts_out, 16)
                        sp.wait_ge(qk_lo_set, c * 2 + 2)
                        sp.dma_start(q_dram[1, :, tok], qk_lo[:, 0, :].bitcast(F32)).then_inc(parts_out, 16)
                        sp.dma_start(k_dram[1, :, tok], qk_lo[:, 1, :].bitcast(F32)).then_inc(parts_out, 16)
                    sp.wait_ge(parts_out, NCH * PARTS_OUT)
                    sp.wait_ge(const_set, 4)

            def load_rows(b, par, half):
                for c in range(PARTS):
                    r = 2 * 32 * half + DK * c
                    for rows, dram, part in ((q_rows, q_dram, c // 2), (k_rows, k_dram, c % 2)):
                        src = dram[part, 64 * half:64 * (half + 1), bass.ds(b * S, S)]
                        sp.dma_start(rows[r:r + DK, par, :, :].bitcast(F32),
                                     src.rearrange("(t d) n -> d t n", d=DK)).then_inc(rows_in[half][par], 16)

            def load_mrow(b, par, half):
                sp.wait_ge(mrow_set, b * 2 + 1 + half)
                r = 64 * half + KROWS
                sp.dma_start(q_rows[r:r + 1, par, :, :].bitcast(F32), mrow[:, half, :].bitcast(F32)).then_inc(mrow_in[half], 16)

            for b in range(2):
                for half in range(2):
                    load_rows(b, b, half)
            load_mrow(0, 0, 0)

            def batch(b, par, more=True, ahead=True):
                load_mrow(b, par, 1)
                if ahead:
                    sp.wait_ge(st_ready, b * PAIRS + PAIRS // 2)
                    load_rows(b + 2, par, 0)
                if more:
                    load_mrow(b + 1, 1 - par, 0)
                if ahead:
                    sp.wait_ge(st_ready, b * PAIRS + PAIRS)
                    load_rows(b + 2, par, 1)

            with sp.Fori(0, (B - 2) // 2) as i:
                batch(i * 2, 0)
                batch(i * 2 + 1, 1)
            batch(B - 2, 0, ahead=False)
            batch(B - 1, 1, more=False, ahead=False)
            ov = out.rearrange("(t p) d -> p t d", p=P)
            for dst, src in ((w1_sb[:, :], w1), (w2_sb[:, :], w2), (h1_sb[:, :, :], h1), (h2_sb[:, :, :], h2),
                             (w3_sb[:, :, :], w3), (hs[:, 0, :], s1), (hs[:, 1, :], s2), (hs[:, 2, :], h1s),
                             (hs[:, 3, :], h2s)):
                sp.dma_start(dst, src).then_inc(ffn_w_in, 16)
            with sp.Fori(0, NCH) as c:
                sp.wait_ge(out_set, c + 1)
                sp.dma_start(ov[:, bass.ds(c * TPC, TPC), :], xs[:, bass.ds(c * TPC, TPC), :]).then_inc(out_done, 16)
            sp.wait_ge(out_done, NCH * 16)

        @block.gpsimd
        def _(pool):
            nc.gpsimd.memset(mhalf[:, :], -0.5).then_inc(const_set, 1)
            pool.wait_ge(const_set, 1)
            nc.gpsimd.memset(vx[:, :, :, DK:VC], 1.0).then_inc(const_set, 1)
            for n, r in ((2, KROWS), (3, 64 + KROWS)):
                pool.wait_ge(const_set, n)
                nc.gpsimd.memset(k_rows[r:r + 1, :, :, :].bitcast(F32), 1.0).then_inc(const_set, 1)

            def inv_std(n, width):
                pool.wait_ge(var_set, n)
                nc.gpsimd.tensor_tensor(rstd[:, 0:width], mv[:, 0:width, 1], mhalf[:, 0:width],
                                        ALU.pow).then_inc(rstd_set, 1)

            pool.wait_ge(const_set, 4)
            with pool.Fori(0, NCH) as c:
                inv_std(c + 1, TPC)
            for g in range(4):
                pool.wait_ge(bias_hi_set, g + 1)
                nc.gpsimd.tensor_tensor(bias_lo[:, 4 * g:4 * g + 4, :], reverse_rows(bias_raw[:, g % 2, :, :]),
                                        bias_hi[:, 4 * g:4 * g + 4, :].bitcast(F32),
                                        ALU.subtract).then_inc(bias_lo_set, 1)
            pool.wait_ge(v_set, NCH)

            def keep_near(b, par):
                nc.gpsimd.tensor_copy(v_near[:, par, :, :, :],
                                      vx[:, bass.ds(b * TPB, TPB), :, :]).then_inc(v_near_set, 1)

            keep_near(0, 0)
            keep_near(1, 1)

            def batch(b, par):
                pool.wait_ge(pv_ready, b * GROUPS + GROUPS)
                keep_near(b + 2, par)
                inv_std(b * 2 + NCH + 1, TPB)
                inv_std(b * 2 + NCH + 2, TPB)

            with pool.Fori(0, (B - 2) // 2) as i:
                batch(i * 2, 0)
                batch(i * 2 + 1, 1)
            for b in (B - 2, B - 1):
                inv_std(b * 2 + NCH + 1, TPB)
                inv_std(b * 2 + NCH + 2, TPB)
            with pool.Fori(0, NCH) as c:
                inv_std(c + NCH + 2 * B + 1, TPC)

        @block.vector
        def _(dve):
            nc.vector.memset(pv[:, :], 0.0).then_inc(psum_zeroed, 1)
            dve.wait_ge(qkv_w_in, 160)
            nc.vector.tensor_copy(identr[:, :], ident[:, :]).then_inc(identr_set, 1)

            held = [0]

            def hold(semaphore, value):
                dve.wait_ge(semaphore, value)
                if not isinstance(value, int):
                    held[0] += 1
                    nc.vector.memset(pad[0:1, held[0] % PADS:held[0] % PADS + 1], 0.0)

            def moments(src, tiles, base):
                for t in range(tiles):
                    last = nc.vector.bn_stats(stats[:, t, :], src(t))
                last.then_inc(dve_order, 1)
                hold(dve_order, base + 1)
                for t in range(tiles):
                    last = nc.vector.bn_aggr(mv[:, t, :], stats[:, t, :])
                last.then_inc(dve_order, 1)
                dve.wait_ge(dve_order, base + 2)
                nc.vector.tensor_scalar(mv[:, 0:tiles, 1], mv[:, 0:tiles, 1], EPS, None, ALU.add).then_inc(var_set, 1)

            def normalize(dst, src, t):
                return nc.vector.tensor_scalar(dst, src, mv[:, t, 0:1], rstd[:, t:t + 1], ALU.subtract, ALU.mult)

            scale = float(1.0 / DK ** 0.5)
            dve.wait_ge(x_in, NCH * 16)
            dve.wait_ge(const_set, 4)

            def chunk(c, first=False):
                tile = lambda t: xs[:, bass.ds(c * TPC + t, 1), :].rearrange("p o d -> p (o d)")
                moments(tile, TPC, c * 2)
                dve.wait_ge(rstd_set, c + 1)
                if not first:
                    dve.wait_ge(xnT_ready, c)
                for t in range(TPC):
                    last = normalize(xn[:, t, :], tile(t), t)
                last.then_inc(xn_set, 1)
                if not first:
                    dve.wait_ge(qk_hi_set, c * 2)
                for i, ready in ((0, q_ready), (1, k_ready)):
                    dve.wait_ge(ready, c + 1)
                    nc.vector.tensor_scalar(qk_f[:, i, :], bank[1 + i], bq_sb[:, i:i + 1], scale if i == 0 else 1.0,
                                            ALU.add, ALU.mult).then_inc(qk_f_set, 1)
                dve.wait_ge(v_ready, c + 1)
                nc.vector.tensor_tensor(
                    vx[:, bass.ds(c * TPC, TPC), :, 0:DK],
                    bank[3].rearrange("p (t h d) -> p t h d", t=TPC, h=H),
                    bv_bc[:, :].rearrange("p (o h d) -> p o h d", o=1, h=H).broadcast_to((P, TPC, H, DK)),
                    ALU.add).then_inc(v_set, 1)
                if not first:
                    dve.wait_ge(parts_out, c * PARTS_OUT)
                for i in range(2):
                    dve.wait_ge(qk_hi_set, c * 2 + (i + 1))
                    nc.vector.tensor_tensor(qk_lo[:, i, :], qk_f[:, i, :], qk_hi[:, i, :].bitcast(F32),
                                            ALU.subtract).then_inc(qk_lo_set, 1)

            chunk(0, first=True)
            with dve.Fori(1, NCH) as c:
                chunk(c)
            dve.wait_ge(max_bias_in, 16)

            def maxima(b, s):
                for it in range(TPB):
                    hold(ms_ready, b * (2 * PAIRS) + (2 * s + it + 1))
                    for k in range(2):
                        h = 2 * s + k
                        col = P - it * P
                        last = nc.vector.tensor_tensor_reduce(
                            out=ms[it][:, k, :], in0=ms[it][:, k, :], in1=reverse(bias_max[:, h, WIN - S - col:WIN - col]), scale=1.0,
                            scalar=-3.4e38, op0=ALU.add, op1=ALU.max, accum_out=mx[:, it, h:h + 1])
                    last.then_inc(ms_read, 1)

            base = 2 * NCH

            def weigh(b, it):
                dve.wait_ge(o_ready, b * TPB + it + 1)
                heads = misc[:, :].rearrange("p (h c) -> p h c", h=H)
                n = b * 6 + base + 1 + it
                nc.vector.reciprocal(rsum[:, :], heads[:, :, DK]).then_inc(dve_order, 1)
                dve.wait_ge(dve_order, n)
                nc.vector.tensor_tensor(
                    on[:, it, :].rearrange("p (h d) -> p h d", h=H), heads[:, :, 0:DK],
                    rsum[:, :].rearrange("p (h o) -> p h o", o=1).broadcast_to((P, H, DK)),
                    ALU.mult).then_inc(on_set, 1)

            def attn_moments(b):
                dve.wait_ge(y_ready, b + 1)
                nc.vector.tensor_tensor(y[:, :, :], misc[:, 0:TPB * D].rearrange("p (t d) -> p t d", t=TPB),
                                        bo_bc[:, :].rearrange("p (o d) -> p o d", o=1).broadcast_to((P, TPB, D)),
                                        ALU.add).then_inc(y_read, 1)
                hold(y_read, b + 1)
                moments(lambda t: y[:, t, :], TPB, b * 6 + base + 2)

            def residual(b, tile):
                dve.wait_ge(rstd_set, b * 2 + NCH + 1)
                for t in range(TPB):
                    last = normalize(y[:, t, :], y[:, t, :], t)
                last.then_inc(y_norm, 1)
                dve.wait_ge(y_norm, b + 1)
                xb = xs[:, bass.ds(b * TPB, TPB), :] if not isinstance(b, int) else xs[:, TPB * b:TPB * b + TPB, :]
                nc.vector.tensor_tensor(xb, xb, y[:, :, :], ALU.add).then_inc(x1_set, 1)
                hold(x1_set, b + 1)
                moments(lambda t: xs[:, bass.ds(b * TPB + t, 1), :].rearrange("p o d -> p (o d)"), TPB,
                        b * 6 + base + 4)

            def second_norm(b):
                dve.wait_ge(rstd_set, b * 2 + NCH + 2)
                if not (isinstance(b, int) and b == 0):
                    dve.wait_ge(zT_ready, b)
                for t in range(TPB):
                    last = normalize(z[:, t, :], xs[:, bass.ds(b * TPB + t, 1), :].rearrange("p o d -> p (o d)"), t)
                last.then_inc(z_set, 1)

            for s in range(PAIRS):
                maxima(0, s)

            def batch(b, par, post=True, more=True):
                for s in range(PAIRS):
                    if post:
                        if s in (2, 3):
                            weigh(b - 1, s - 2)
                        if s == 5:
                            attn_moments(b - 1)
                        if s == 6:
                            residual(b - 1, None)
                        if s == 7:
                            second_norm(b - 1)
                    if more:
                        maxima(b + 1, s)

            batch(0, 0, post=False)
            with dve.Fori(0, (B - 2) // 2) as i:
                batch(i * 2 + 1, 1)
                batch(i * 2 + 2, 0)
            batch(B - 1, 1, more=False)
            weigh(B - 1, 0)
            weigh(B - 1, 1)
            attn_moments(B - 1)
            residual(B - 1, None)
            second_norm(B - 1)

            dve.wait_ge(ffn_w_in, 144)
            with dve.Fori(0, NCH) as c:
                for k in range(NK):
                    dve.wait_ge(silu_done, c * NK + (k + 1))
                    nc.vector.scalar_tensor_tensor(
                        out=g0[:, k, bass.ds(c * CH, CH)], in0=bank[2 * k + 1], scalar=hs[:, 1, k:k + 1],
                        in1=gate[:, k % 2, :], op0=ALU.mult, op1=ALU.mult).then_inc(g0_set, 1)
            base3 = base + 6 * B

            def last_norm(c, first=False):
                if not first:
                    dve.wait_ge(out_set, c)
                dve.wait_ge(y3_ready, c + 1)
                nc.vector.tensor_tensor(xn[:, :, :], bank[7].rearrange("p (t d) -> p t d", t=TPC),
                                        w3s_bc[:, :].rearrange("p (o d) -> p o d", o=1).broadcast_to((P, TPC, D)),
                                        ALU.mult).then_inc(y3_read, 1)
                hold(y3_read, c + 1)
                moments(lambda t: xn[:, t, :], TPC, c * 2 + base3)
                dve.wait_ge(rstd_set, c + (NCH + 2 * B + 1))
                for t in range(TPC):
                    last = normalize(xn[:, t, :], xn[:, t, :], t)
                last.then_inc(y3_norm, 1)
                dve.wait_ge(y3_norm, c + 1)
                xc = xs[:, bass.ds(c * TPC, TPC), :]
                nc.vector.tensor_tensor(xc, xc, xn[:, :, :], ALU.add).then_inc(out_set, 1)

            last_norm(0, first=True)
            with dve.Fori(1, NCH) as c:
                last_norm(c)

        @block.scalar
        def _(act):
            def chunk(c, first=False):
                act.wait_ge(xnT_ready, c + 1)
                if not first:
                    act.wait_ge(v_ready, c)
                nc.scalar.copy(xT[:, :], bank[0]).then_inc(xT_set, 1)
                if not first:
                    act.wait_ge(parts_out, c * PARTS_OUT)
                for i in range(2):
                    act.wait_ge(qk_f_set, c * 2 + (i + 1))
                    nc.scalar.copy(qk_hi[:, i, :], qk_f[:, i, :]).then_inc(qk_hi_set, 1)

            chunk(0, first=True)
            with act.Fori(1, NCH) as c:
                chunk(c)
            for g in range(4):
                act.wait_ge(raw_in[g % 2], 16 * (g // 2 + 1))
                nc.scalar.copy(bias_hi[:, 4 * g:4 * g + 4, :], reverse_rows(bias_raw[:, g % 2, :, :])).then_inc(bias_hi_set, 1)

            def minus_max(b, half):
                act.wait_ge(mT_ready, b * 2 + 1 + half)
                if not (isinstance(b, int) and b == 0):
                    act.wait_ge(mrow_in[half], b * 16)
                nc.scalar.mul(mrow[:, half, :], misc[0:HALF, 0:S], -1.0).then_inc(mrow_set, 1)

            def probabilities(b, s, first=False):
                act.wait_ge(st_ready, b * PAIRS + (s + 1))
                if not (first and s < PRING):
                    act.wait_ge(pv_ready, b * GROUPS + ((s - PRING) // 2 + 1))
                nc.scalar.activation(probs[:, s % PRING, :, :, :].rearrange("p k j n -> p (k j n)"),
                                     st[s % 2][:, :, :].rearrange("p k n -> p (k n)"), ACT.Exp).then_inc(exp_done, 1)

            def keep_weighted(b, par, g):
                act.wait_ge(pv_ready, b * GROUPS + (g + 1))
                nc.scalar.copy(oT[:, par, g, :], pv[:, 0:S]).then_inc(oT_set, 1)

            def keep_onT(b):
                act.wait_ge(onT_ready, b + 1)
                nc.scalar.copy(onT[:, :], misc[:, 0:S]).then_inc(onT_set, 1)

            def keep_zT(b):
                act.wait_ge(zT_ready, b + 1)
                nc.scalar.copy(zT[:, bass.ds(b * S, S)], misc[:, 0:S]).then_inc(zT_set, 1)

            minus_max(0, 0)

            def batch(b, par, first=False, more=True):
                for s in range(PAIRS):
                    if s == 1:
                        minus_max(b, 1)
                    if s == 4 and not first:
                        keep_onT(b - 1)
                    if s == 6 and more:
                        minus_max(b + 1, 0)
                    probabilities(b, s, first)
                    if s == 0 and not first:
                        keep_weighted(b - 1, 1 - par, GROUPS - 1)
                    if s >= 2 and s % 2 == 0:
                        keep_weighted(b, par, s // 2 - 1)
                if not first:
                    keep_zT(b - 1)

            batch(0, 0, first=True)
            with act.Fori(0, (B - 2) // 2) as i:
                batch(i * 2 + 1, 1)
                batch(i * 2 + 2, 0)
            batch(B - 1, 1, more=False)
            keep_weighted(B - 1, 1, GROUPS - 1)
            keep_onT(B - 1)
            keep_zT(B - 1)

            act.wait_ge(ffn_w_in, 144)

            def gates(c, first=False):
                for k in range(NK):
                    act.wait_ge(up_ready, c * NK + (k + 1))
                    if not (first and k < 2):
                        act.wait_ge(g0_set, c * NK + (k - 1))
                    nc.scalar.activation(gate[:, k % 2, :], bank[2 * k], ACT.Silu,
                                         scale=hs[:, 0, k:k + 1]).then_inc(silu_done, 1)

            gates(0, first=True)
            with act.Fori(1, NCH) as c:
                gates(c)
            with act.Fori(0, NCH) as c:
                for i, (ready, dst, done) in enumerate(((a1_ready, a1, a1_set), (a2_ready, a2, a2_set))):
                    for k in range(NK):
                        act.wait_ge(ready, c * NK + (k + 1))
                        nc.scalar.activation(dst[:, k, :], bank[HBANK[i][k]], ACT.Gelu,
                                             scale=hs[:, 2 + i, k:k + 1]).then_inc(done, 1)

        @block.tensor
        def _(pe):
            mm = nc.tensor.matmul
            pe.wait_ge(qkv_w_in, 160)

            def chunk(c, first=False):
                pe.wait_ge(xn_set, c + 1)
                if not first:
                    pe.wait_ge(xT_set, c)
                for t in range(TPC):
                    last = nc.tensor.transpose(bank[0][:, t * P:(t + 1) * P], xn[:, t, :], ident[:, :])
                last.then_inc(xnT_ready, 1)
                pe.wait_ge(xT_set, c + 1)
                if not first:
                    pe.wait_ge(qk_f_set, c * 2)
                mm(bank[1], wq_sb[:, :], xT[:, :], start=True, stop=True).then_inc(q_ready, 1)
                mm(bank[2], wk_sb[:, :], xT[:, :], start=True, stop=True).then_inc(k_ready, 1)
                if not first:
                    pe.wait_ge(v_set, c)
                for t in range(TPC):
                    last = mm(bank[3][:, t * P:(t + 1) * P], xT[:, t * P:(t + 1) * P], wv_sb[:, :],
                              start=True, stop=True)
                last.then_inc(v_ready, 1)

            chunk(0, first=True)
            with pe.Fori(1, NCH) as c:
                chunk(c)

            def rows(r, par, h, extra):
                r0 = 64 * (h // HALF)
                return r[r0:r0 + KROWS + extra, par, h % HALF, :]

            def max_scores(b, par, s, first=False):
                if s % (PAIRS // 2) == 0:
                    pe.wait_ge(rows_in[s // (PAIRS // 2)][par], b * (ROW_DMAS * 8) + ROW_DMAS * (16 - 8 * par))
                for it in range(TPB):
                    if not (first and s == 0):
                        pe.wait_ge(ms_read, b * (2 * PAIRS) + (2 * s + it - 1))
                    for k in range(2):
                        h = 2 * s + k
                        last = mm(ms[it][:, k, :], rows(q_rows, par, h, 0)[:, it * P:(it + 1) * P],
                                  rows(k_rows, par, h, 0), start=True, stop=True)
                    last.then_inc(ms_ready, 1)

            def maxima_T(b, half):
                pe.wait_ge(ms_read, b * (2 * PAIRS) + PAIRS * (half + 1))
                for it in range(TPB):
                    last = mm(misc[0:HALF, it * P:(it + 1) * P], mx[:, it, half * HALF:(half + 1) * HALF],
                              ident[:, :], start=True, stop=True)
                last.then_inc(mT_ready, 1)

            def scores(b, par, s, first=False):
                if s % (PAIRS // 2) == 0:
                    pe.wait_ge(mrow_in[s // (PAIRS // 2)], b * 16 + 16)
                if not (first and s < 2):
                    pe.wait_ge(exp_done, b * PAIRS + (s - 1))
                for k in range(2):
                    h = 2 * s + k
                    o = st[s % 2][:, k, :]
                    mm(o, identr[:, :], windows(bias_hi[:, h, :], 0, P, 2, S), start=True, stop=False)
                    mm(o, identr[:, :], windows(bias_lo[:, h, :], 0, P, 2, S), start=False, stop=False)
                    for j, jt in enumerate((1, 0)):
                        last = mm(o[:, j * S:(j + 1) * S], rows(k_rows, par, h, 1)[:, jt * P:(jt + 1) * P],
                                  rows(q_rows, par, h, 1), start=False, stop=(j == 1))
                last.then_inc(st_ready, 1)

            def weighted(b, par, g, first=False):
                pe.wait_ge(exp_done, b * PAIRS + (2 * g + 2))
                if g == 0:
                    pe.wait_ge(v_near_set, b + 1)
                if not (first and g == 0):
                    pe.wait_ge(oT_set, b * GROUPS + g)
                for j, jt in enumerate((1, 0)):
                    for r in range(4):
                        h = 4 * g + r
                        last = mm(pv[32 * r:32 * r + VC, 0:S], v_near[:, par, jt, h, :],
                                  probs[:, (2 * g + r // 2) % PRING, r % 2, j, :], start=(j == 0), stop=(j == 1))
                last.then_inc(pv_ready, 1)

            def back(b, par, it):
                if it == 0:
                    pe.wait_ge(oT_set, b * GROUPS + GROUPS)
                else:
                    pe.wait_ge(on_set, b * TPB + it)
                for g in range(GROUPS):
                    last = nc.tensor.transpose(misc[:, g * P:(g + 1) * P], oT[:, par, g, it * P:(it + 1) * P],
                                               ident[:, :])
                last.then_inc(o_ready, 1)

            def heads_T(b):
                pe.wait_ge(on_set, b * TPB + TPB)
                for it in range(TPB):
                    last = nc.tensor.transpose(misc[:, it * P:(it + 1) * P], on[:, it, :], ident[:, :])
                last.then_inc(onT_ready, 1)

            def project(b):
                pe.wait_ge(onT_set, b + 1)
                for it in range(TPB):
                    last = mm(misc[:, it * P:(it + 1) * P], onT[:, it * P:(it + 1) * P], wo_sb[:, :],
                              start=True, stop=True)
                last.then_inc(y_ready, 1)

            def norm_T(b):
                pe.wait_ge(z_set, b + 1)
                for it in range(TPB):
                    last = nc.tensor.transpose(misc[:, it * P:(it + 1) * P], z[:, it, :], ident[:, :])
                last.then_inc(zT_ready, 1)

            pe.wait_ge(qk_f_set, 2 * NCH)
            pe.wait_ge(v_set, NCH)
            for s in range(PAIRS):
                max_scores(0, 0, s, first=True)
            maxima_T(0, 0)
            pe.wait_ge(identr_set, 1)
            pe.wait_ge(bias_hi_set, 4)
            pe.wait_ge(bias_lo_set, 4)
            pe.wait_ge(psum_zeroed, 1)

            def batch(b, par, first=False, more=True):
                for s in range(PAIRS):
                    if more:
                        max_scores(b + 1, 1 - par, s)
                    if s == 1:
                        if first:
                            pe.wait_ge(mrow_set, 1)
                        else:
                            pe.wait_ge(oT_set, b * GROUPS)
                        maxima_T(b, 1)
                    scores(b, par, s, first)
                    if s == 0 and not first:
                        weighted(b - 1, 1 - par, GROUPS - 1)
                    if s >= 2 and s % 2 == 0:
                        weighted(b, par, s // 2 - 1, first)
                    if s == 1 and not first:
                        pe.wait_ge(mrow_set, b * 2 + 2)
                        back(b - 1, 1 - par, 0)
                    if s == 2 and not first:
                        back(b - 1, 1 - par, 1)
                    if s == 3 and not first:
                        heads_T(b - 1)
                    if s == 4 and not first:
                        project(b - 1)
                    if s == 5 and more:
                        if first:
                            pe.wait_ge(mrow_set, 2)
                        else:
                            pe.wait_ge(y_read, b)
                        maxima_T(b + 1, 0)
                    if s == 7 and not first:
                        if more:
                            pe.wait_ge(mrow_set, b * 2 + 3)
                        else:
                            pe.wait_ge(y_read, b)
                        norm_T(b - 1)

            batch(0, 0, first=True)
            with pe.Fori(0, (B - 2) // 2) as i:
                batch(i * 2 + 1, 1)
                batch(i * 2 + 2, 0)
            batch(B - 1, 1, more=False)
            weighted(B - 1, 1, GROUPS - 1)
            pe.wait_ge(zT_set, B - 1)
            back(B - 1, 1, 0)
            back(B - 1, 1, 1)
            heads_T(B - 1)
            project(B - 1)
            pe.wait_ge(y_read, B)
            norm_T(B - 1)

            pe.wait_ge(ffn_w_in, 144)
            pe.wait_ge(exp_done, B * PAIRS)
            pe.wait_ge(ms_read, B * 2 * PAIRS)
            pe.wait_ge(oT_set, B * GROUPS)
            pe.wait_ge(zT_set, B)

            def gates(c, first=False):
                for k in range(NK):
                    if not first:
                        pe.wait_ge(g0_set, c * NK + (k - NK + 1))
                    zc = zT[:, bass.ds(c * CH, CH)]
                    mm(bank[2 * k], w1_sb[:, k * P:(k + 1) * P], zc, start=True, stop=True)
                    mm(bank[2 * k + 1], w2_sb[:, k * P:(k + 1) * P], zc, start=True, stop=True).then_inc(up_ready, 1)

            gates(0, first=True)
            with pe.Fori(1, NCH) as c:
                gates(c)
            pe.wait_ge(g0_set, NCH * NK)

            def layer1(c, first=False):
                for k in range(NK):
                    if not first:
                        if k < 3:
                            pe.wait_ge(a1_set, c * NK + (k - NK + 1))
                        else:
                            pe.wait_ge(a2_set, c * NK)
                    for j in range(NK):
                        last = mm(bank[HBANK[0][k]], h1_sb[:, j, k * P:(k + 1) * P], g0[:, j, bass.ds(c * CH, CH)],
                                  start=(j == 0), stop=(j == NK - 1))
                    last.then_inc(a1_ready, 1)

            def layer2(c, first=False):
                pe.wait_ge(a1_set, c * NK + NK)
                for k in range(NK):
                    if not first and k < 3:
                        pe.wait_ge(a2_set, c * NK + (k - NK + 1))
                    for j in range(NK):
                        last = mm(bank[HBANK[1][k]], h2_sb[:, j, k * P:(k + 1) * P], a1[:, j, :],
                                  start=(j == 0), stop=(j == NK - 1))
                    last.then_inc(a2_ready, 1)

            def layer3(c, first=False):
                pe.wait_ge(a2_set, c * NK + NK)
                if not first:
                    pe.wait_ge(y3_read, c)
                for t in range(TPC):
                    for j in range(NK):
                        last = mm(bank[7][:, t * P:(t + 1) * P], a2[:, j, t * P:(t + 1) * P], w3_sb[:, j, :],
                                  start=(j == 0), stop=(j == NK - 1))
                last.then_inc(y3_ready, 1)

            layer1(0, first=True)
            layer2(0, first=True)
            layer1(1)
            layer3(0, first=True)
            layer2(1)
            with pe.Fori(2, NCH) as c:
                layer1(c)
                layer3(c - 1)
                layer2(c)
            layer3(NCH - 1)

    return nc


def kernel(**inputs):
    import numpy as np
    import concourse.bacc as bacc
    from concourse.bass_utils import run_bass_kernel_spmd

    a = {k.removeprefix("L0_"): np.asarray(v) for k, v in inputs.items()}
    w = a["attn_W_qkv"]
    bqkv = a["attn_b_qkv"]
    rel = np.ascontiguousarray(a["attn_rel_bias"].T)
    pad = ((0, 0), (P - 1, EXT - REL - (P - 1)))
    col = lambda v: v.reshape(-1, 1)
    tiles = lambda v: v.reshape(NK, P).T
    weights = lambda m, n: m.T.reshape(NK, P, n).transpose(1, 0, 2)
    arrays = {
        "x": a["attn_x"].reshape(TOK, D),
        "wq": w[:, 0:D], "wk": w[:, D:2 * D], "wv": w[:, 2 * D:3 * D],
        "bq": col(bqkv[0:D]), "bk": col(bqkv[D:2 * D]), "bv": bqkv[None, 2 * D:3 * D],
        "wo": a["attn_W_out"], "bo": a["attn_b_out"][None, :],
        "ext": np.pad(rel, pad, mode="edge")[:, ::-1], "ext_max": np.pad(rel[:, ::-1], pad, mode="edge")[:, ::-1],
        "w1": a["ffn_w1_w"].T, "s1": tiles(a["ffn_w1_s"]), "w2": a["ffn_w2_w"].T, "s2": tiles(a["ffn_w2_s"]),
        "h1": weights(a["ffn_h1_w"], HID), "h1s": tiles(a["ffn_h1_s"]),
        "h2": weights(a["ffn_h2_w"], HID), "h2s": tiles(a["ffn_h2_s"]),
        "w3": weights(a["ffn_w3_w"], D), "w3s": a["ffn_w3_s"][None, :],
        "ident_in": np.eye(P, dtype=np.float32),
    }
    arrays = {k: np.ascontiguousarray(v) for k, v in arrays.items()}
    nc = bacc.Bacc("TRN2", target_bir_lowering=False, num_devices=1)
    args = [nc.dram_tensor(k, v.shape, mybir.dt.from_np(v.dtype), kind="ExternalInput").ap() for k, v in arrays.items()]
    out = nc.dram_tensor("out", (TOK, D), F32, kind="ExternalOutput").ap()
    build(nc, *args, out)
    r = run_bass_kernel_spmd(nc, [arrays], core_ids=[0])
    return r.results[0]["out"].reshape(B, S, D)
```

```python
import concourse.bass as bass
from concourse import mybir
from contextlib import ExitStack

F32 = mybir.dt.float32
F32R = mybir.dt.float32r
I32 = mybir.dt.int32
AX = mybir.AxisListType
ALU = mybir.AluOpType
ACT = mybir.ActivationFunctionType

B, S, D = 8, 256, 128
H, DK = 16, 8
HID = 512
P = 128
EPS = 1e-5
TOK = B * S
NT = TOK // P
TPB = S // P
MAX_REL = 128
REL = 2 * MAX_REL + 1
WIN = P + S
EXT = WIN + P - 1
CH = 512
NCH = TOK // CH
TPC = CH // P
NK = HID // P
PAIRS = H // 2
GROUPS = H // 4
HALF = H // 2
PARTS = 4
KROWS = PARTS * DK
VC = DK + 1
PADS = 128
PRING = 4
W1, W2, W_H1, W_H2, W3 = 0, HID, 2 * HID, 2 * HID + NK * HID, 2 * HID + 2 * NK * HID
WCOLS = W3 + NK * D
WPIECE = 512


def windows(ap, start, step, count, width):
    return bass.AP(tensor=ap.tensor, offset=ap.offset + start, ap=[list(ap.ap[0]), [step, count], [1, width]])


def reverse(ap):
    n = ap.shape[-1]
    return bass.AP(tensor=ap.tensor, offset=ap.offset + n - 1, ap=[list(ap.ap[0]), [-1, n]])


def reverse_rows(ap):
    (row, m), (_, n) = ap.ap[1], ap.ap[2]
    return bass.AP(tensor=ap.tensor, offset=ap.offset + n - 1, ap=[list(ap.ap[0]), [row, m], [-1, n]])


def twice(ap):
    return bass.AP(tensor=ap.tensor, offset=ap.offset, ap=[list(ap.ap[0]), [0, 2], list(ap.ap[1])])


def build(nc, x, wq, wk, wv, bq, bk, bv, wo, bo, ext, ext_max, w1, s1, w2, s2, h1, h1s, h2, h2s, w3, w3s,
          ident_in, out):
    ctx = ExitStack()
    with ctx:
        def sb(name, shape, dt=F32):
            return ctx.enter_context(nc.sbuf_tensor(name, shape, dt))

        def sem(name):
            return ctx.enter_context(nc.semaphore(name))

        ident = sb("ident", [P, P])
        identr = sb("identr", [P, P], F32R)
        wq_sb = sb("wq_sb", [P, D])
        wk_sb = sb("wk_sb", [P, D])
        wv_sb = sb("wv_sb", [P, D])
        wo_sb = sb("wo_sb", [P, D])
        bq_sb = sb("bq_sb", [P, 2])
        bv_bc = sb("bv_bc", [P, D])
        bo_bc = sb("bo_bc", [P, D])
        xs = sb("xs", [P, NT, D])
        stats = sb("stats", [P, TPC, 6])
        mv = sb("mv", [P, NT, 2])
        rstd = sb("rstd", [P, NT])
        mhalf = sb("mhalf", [P, TPC])
        xn = sb("xn", [P, TPC, D])
        xT = sb("xT", [P, CH])
        z_parts = sb("z_parts", [P, 2, TOK], F32R)
        w_hi = sb("w_hi", [P, WCOLS], F32R)
        qk_parts = [view[:, 2 * CH * n:2 * CH * (n + 2)].rearrange("p (a i n) -> p a i n", a=2, i=2)
                    for view in (z_parts[:, :, :].rearrange("p a n -> p (a n)"), w_hi) for n in (0, 2)]
        qk_hi = [parts[:, 0, :, :] for parts in qk_parts]
        qk_lo = [parts[:, 1, :, :] for parts in qk_parts]
        room = sb("room", [P, 2 * NK * (TOK + CH)], F32R)
        table = room[:, 0:2 * H * WIN].rearrange("p (a h c) -> p a h c", a=2, h=H)
        rows_at = 2 * H * WIN
        q_rows = room[:, rows_at:rows_at + 2 * HALF * S].rearrange(
            "p (a h n) -> p a h n", a=2, h=HALF)
        k_rows = room[:, rows_at + 2 * HALF * S:rows_at + 4 * HALF * S].rearrange(
            "p (a h n) -> p a h n", a=2, h=HALF)
        g_parts = room[:, 0:2 * NK * TOK].rearrange("p (a k n) -> p a k n", a=2, k=NK)
        a1_parts = room[:, 2 * NK * TOK:2 * NK * (TOK + CH)].rearrange("p (a k n) -> p a k n", a=2, k=NK)
        vx = sb("vx", [P, NT, H, VC])
        v_near = sb("v_near", [P, 2, TPB, H, VC])
        big = sb("big", [P, NK * TOK])
        bias_max = big[:, 0:H * WIN].rearrange("p (h c) -> p h c", h=H)
        pad = sb("pad", [P, PADS])
        mx = sb("mx", [P, TPB, H])
        mrow = sb("mrow", [HALF, 2, S], F32R)
        ring = sb("ring", [P, PRING * 4 * S])
        probs = ring[:, :].rearrange("p (a k j n) -> p a k j n", a=PRING, k=2, j=2)
        bias_raw = [place[:, at:at + 4 * WIN].rearrange("p (h c) -> p h c", h=4)
                    for place, at in ((ring, 0), (ring, 4 * WIN), (ring, 0), (big, H * WIN))]
        oT = big[:, H * WIN:H * WIN + 2 * GROUPS * S].rearrange(
            "p (a g n) -> p a g n", a=2, g=GROUPS)
        qk_f = big[:, H * WIN:H * WIN + 4 * CH].rearrange("p (a i n) -> p a i n", a=2, i=2)
        rsum = sb("rsum", [P, H])
        on = sb("on", [P, TPB, D])
        onT = sb("onT", [P, S])
        y_and_z = sb("y_and_z", [P, 2 * TPB * D])
        y = y_and_z[:, 0:TPB * D].rearrange("p (t d) -> p t d", t=TPB)
        z = y_and_z[:, TPB * D:2 * TPB * D].rearrange("p (t d) -> p t d", t=TPB)
        w_lo = big[:, 0:WCOLS]
        w_low_max = sb("w_low_max", [P, WCOLS // WPIECE])
        w_low_top = sb("w_low_top", [P, 1])
        w_low_any = sb("w_low_any", [1, 1])
        hs = sb("hs", [P, 4, NK])
        w3s_sb = sb("w3s_sb", [P, 1])
        act_f = ring[:, 0:2 * NK * CH].rearrange("p (a k n) -> p a k n", a=2, k=NK)
        gate = sb("gate", [P, 2, CH])
        y3T = y_and_z[:, 0:CH]

        x_norm = (xn, y_and_z[:, :].rearrange("p (t d) -> p t d", t=TPC))

        st = [ctx.enter_context(nc.psum_tensor(f"st{i}", [P, 2, 2 * S], F32)) for i in range(2)]
        ms = [ctx.enter_context(nc.psum_tensor(f"ms{i}", [P, 2, S], F32)) for i in range(2)]
        pv = ctx.enter_context(nc.psum_tensor("pv", [P, 512], F32))
        misc = ctx.enter_context(nc.psum_tensor("misc", [P, 512], F32))
        bank = [st[0][:, 0, :], st[0][:, 1, :], st[1][:, 0, :], st[1][:, 1, :],
                ms[0][:, :, :].rearrange("p a n -> p (a n)"), ms[1][:, :, :].rearrange("p a n -> p (a n)"),
                pv[:, :], misc[:, :]]

        TBANK, QBANK, KBANK = (0, 4), (1, 5), (2, 7)
        HBANK = ((0, 1, 2, 3), (4, 5, 6, 3))

        q_dram = nc.dram_tensor("q_parts", (2, P, TOK), F32, kind="Internal").ap()
        k_dram = nc.dram_tensor("k_parts", (3, P, TOK), F32, kind="Internal").ap()

        x_in = [sem(f"x_in{c}") for c in range(NCH)]
        qkv_w_in = sem("qkv_w_in")
        out_w_in = sem("out_w_in")
        max_bias_in = [sem(f"max_bias_in{i}") for i in range(2)]
        raw_in = [sem(f"raw_in{i}") for i in range(2)]
        scales_in = sem("scales_in")
        ffn_w_in = [sem(f"ffn_w_in{i}") for i in range(5)]
        const_set = sem("const_set")
        psum_zeroed = sem("psum_zeroed")
        bq_scaled = sem("bq_scaled")
        identr_set = sem("identr_set")
        ones_set = sem("ones_set")
        table_hi_set = sem("table_hi_set")
        table_lo_set = sem("table_lo_set")
        dve_order = sem("dve_order")
        var_set = sem("var_set")
        rstd_set = sem("rstd_set")
        xn_set = sem("xn_set")
        xnT_ready = sem("xnT_ready")
        xT_set = sem("xT_set")
        q_ready = sem("q_ready")
        k_ready = sem("k_ready")
        v_ready = sem("v_ready")
        qk_f_set = sem("qk_f_set")
        qk_hi_set = sem("qk_hi_set")
        qk_lo_set = sem("qk_lo_set")
        v_set = sem("v_set")
        parts_out = [sem(f"parts_out{i}") for i in range(2)]
        rows_in = [[sem(f"rows_in{i}{p}") for p in range(2)] for i in range(2)]
        mrow_in = [sem(f"mrow_in{i}") for i in range(2)]
        ms_ready = sem("ms_ready")
        ms_read = sem("ms_read")
        mT_ready = sem("mT_ready")
        mrow_set = sem("mrow_set")
        st_ready = sem("st_ready")
        exp_done = sem("exp_done")
        pv_ready = sem("pv_ready")
        oT_set = sem("oT_set")
        o_ready = sem("o_ready")
        on_set = sem("on_set")
        onT_ready = sem("onT_ready")
        onT_set = sem("onT_set")
        y_ready = sem("y_ready")
        y_read = sem("y_read")
        y_norm = sem("y_norm")
        x1_set = sem("x1_set")
        v_near_set = sem("v_near_set")
        z_set = sem("z_set")
        zT_ready = sem("zT_ready")
        z_hi_set = sem("z_hi_set")
        z_lo_set = sem("z_lo_set")
        w_hi_set = sem("w_hi_set")
        w_lo_set = sem("w_lo_set")
        w_low_max_set = sem("w_low_max_set")
        w_low_top_set = sem("w_low_top_set")
        w_low_row = sem("w_low_row")
        w_low_any_set = sem("w_low_any_set")
        up_ready = sem("up_ready")
        silu_done = sem("silu_done")
        gate_set = sem("gate_set")
        g_hi_set = sem("g_hi_set")
        g_lo_pool = sem("g_lo_pool")
        g_lo_dve = sem("g_lo_dve")
        a1_ready = sem("a1_ready")
        a1_set = sem("a1_set")
        a1_hi_set = sem("a1_hi_set")
        a1_lo_set = sem("a1_lo_set")
        a2_ready = sem("a2_ready")
        a2_set = sem("a2_set")
        a2_hi_set = sem("a2_hi_set")
        a2_lo_set = sem("a2_lo_set")
        y3_ready = sem("y3_ready")
        y3T_set = sem("y3T_set")
        y3_back = sem("y3_back")
        y3_set = sem("y3_set")
        y3_norm = sem("y3_norm")
        out_set = sem("out_set")
        out_done = sem("out_done")

        block = ctx.enter_context(nc.Block())

        def layer_parts(c, i, k):
            if i == 0:
                return a1_parts[:, 0, k, :], a1_parts[:, 1, k, :]
            tok = bass.ds(c * CH, CH)
            return g_parts[:, 0, k, tok], g_parts[:, 1, k, tok]

        ROW_DMAS = PARTS
        PARTS_OUT = 5 * 16

        def load_table(eng, g):
            eng.dma_start(bias_raw[g][:, :, :],
                          bass.AP(tensor=ext.tensor, offset=4 * g * EXT,
                                  ap=[[1, P], [EXT, 4], [1, WIN]])).then_inc(raw_in[g % 2], 16)

        scale = float(1.0 / DK ** 0.5)

        def matrix_of(piece):
            return sum(piece * WPIECE >= at for at in (W2, W_H1, W_H2, W3))

        WPIECES = WCOLS // WPIECE
        PIECES_AT = ((), (0, 1), (), (2,), (3, 4), (5,), (6, 7), (8, 9, 10))

        @block.sync
        def _(sp):
            xv = x.rearrange("(t p) d -> p t d", p=P)
            for c, (dst, src) in enumerate(((ident, ident_in), (wq_sb, wq), (wk_sb, wk), (wv_sb, wv))):
                sp.dma_start(xs[:, c * TPC:(c + 1) * TPC, :], xv[:, c * TPC:(c + 1) * TPC, :]).then_inc(x_in[c], 16)
                sp.dma_start(dst[:, :], src).then_inc(qkv_w_in, 16)
            def load_bias_max(half):
                sp.dma_start(bias_max[:, HALF * half:HALF * (half + 1), :],
                             bass.AP(tensor=ext_max.tensor, offset=HALF * half * EXT,
                                     ap=[[1, P], [EXT, HALF], [1, WIN]])).then_inc(max_bias_in[half], 16)

            load_bias_max(0)

            def store_parts(c):
                tok = slice(c * CH, (c + 1) * CH)
                sp.wait_ge(qk_hi_set, c * 2 + 2)
                sp.dma_start(q_dram[0, :, tok], qk_hi[c][:, 0, :].bitcast(F32)).then_inc(parts_out[c > 0], 16)
                for plane in (0, 2):
                    sp.dma_start(k_dram[plane, :, tok], qk_hi[c][:, 1, :].bitcast(F32)).then_inc(parts_out[c > 0], 16)
                sp.wait_ge(qk_lo_set, c * 2 + 2)
                sp.dma_start(q_dram[1, :, tok], qk_lo[c][:, 0, :].bitcast(F32)).then_inc(parts_out[c > 0], 16)
                sp.dma_start(k_dram[1, :, tok], qk_lo[c][:, 1, :].bitcast(F32)).then_inc(parts_out[c > 0], 16)

            def load_rows(b, par, half):
                for c in range(0, PARTS, 2):
                    r = 2 * 32 * half + DK * c
                    for rows, dram, part in ((q_rows, q_dram, 0), (k_rows, k_dram, c // 2)):
                        src = bass.AP(tensor=dram.tensor, offset=(part * P + half * HALF) * TOK + b * S,
                                      ap=[[H * TOK, 2 * DK], [TOK, HALF], [1, S]])
                        sp.dma_start(rows[r:r + 2 * DK, par, :, :].bitcast(F32), src).then_inc(rows_in[half][par], 16)

            def load_mrow(b, par, half):
                sp.wait_ge(mrow_set, b * 2 + 1 + half)
                r = 64 * half + KROWS
                sp.dma_start(q_rows[r:r + 1, par, :, :].bitcast(F32), mrow[:, half, :].bitcast(F32)).then_inc(mrow_in[half], 16)

            store_parts(0)
            sp.wait_ge(parts_out[0], PARTS_OUT)
            for half in range(2):
                load_rows(0, 0, half)
            load_bias_max(1)
            sp.wait_ge(table_lo_set, 1)
            load_table(sp, 2)
            for half in range(2):
                load_rows(1, 1, half)
            sp.wait_ge(qk_hi_set, NCH * 2)
            sp.wait_ge(qk_lo_set, NCH * 2)
            load_table(sp, 3)
            load_mrow(0, 0, 0)
            for c in range(1, NCH):
                store_parts(c)
            sp.wait_ge(parts_out[1], (NCH - 1) * PARTS_OUT)

            def batch(b, par, more=True, ahead=True):
                load_mrow(b, par, 1)
                if ahead:
                    sp.wait_ge(st_ready, b * PAIRS + PAIRS // 2)
                    load_rows(b + 2, par, 0)
                if more:
                    load_mrow(b + 1, 1 - par, 0)
                if ahead:
                    sp.wait_ge(st_ready, b * PAIRS + PAIRS)
                    load_rows(b + 2, par, 1)

            with sp.Fori(0, (B - 2) // 2) as i:
                batch(i * 2, 0)
                batch(i * 2 + 1, 1)
            batch(B - 2, 0, ahead=False)
            batch(B - 1, 1, more=False, ahead=False)
            ov = out.rearrange("(t p) d -> p t d", p=P)
            for i, (dst, src) in enumerate(((hs[:, 0, :], s1), (hs[:, 1, :], s2), (hs[:, 2, :], h1s), (hs[:, 3, :], h2s),
                                              (w3s_sb[:, :], w3s))):
                sp.dma_start(dst, src).then_inc(scales_in, 16)
            sp.wait_ge(ms_read, B * 2 * PAIRS)
            for i, (at, src) in enumerate(((W1, w1), (W2, w2), (W_H1, h1), (W_H2, h2), (W3, w3))):
                sp.dma_start(w_lo[:, at:at + src.shape[-1]], src).then_inc(ffn_w_in[i], 16)
            with sp.Fori(0, NCH) as c:
                sp.wait_ge(out_set, c + 1)
                sp.dma_start(ov[:, bass.ds(c * TPC, TPC), :], xs[:, bass.ds(c * TPC, TPC), :]).then_inc(out_done, 16)
            sp.wait_ge(out_done, NCH * 16)

        @block.gpsimd
        def _(pool):
            nc.gpsimd.memset(mhalf[:, :], -0.5).then_inc(const_set, 1)
            pool.wait_ge(const_set, 1)

            def inv_std(n, width, at=0):
                pool.wait_ge(var_set, n)
                nc.gpsimd.tensor_tensor(rstd[:, at:at + width], mv[:, at:at + width, 1], mhalf[:, 0:width],
                                        ALU.pow).then_inc(rstd_set, 1)

            for c in range(NCH):
                inv_std(c + 1, TPC, c * TPC)
                if c == 0:
                    nc.gpsimd.memset(vx[:, :, :, DK:VC], 1.0).then_inc(const_set, 1)
            pool.wait_ge(rstd_set, NCH)
            nc.gpsimd.memset(k_rows[KROWS:KROWS + 1, :, :, :].bitcast(F32), 1.0).then_inc(ones_set, 1)
            pool.wait_ge(ones_set, 1)
            r = 64 + KROWS
            nc.gpsimd.memset(k_rows[r:r + 1, :, :, :].bitcast(F32), 1.0).then_inc(ones_set, 1)
            pool.wait_ge(ones_set, 2)
            for g in range(GROUPS):
                pool.wait_ge(table_hi_set, g + 1)
                nc.gpsimd.tensor_tensor(table[:, 1, 4 * g:4 * g + 4, :], reverse_rows(bias_raw[g][:, :, :]),
                                        table[:, 0, 4 * g:4 * g + 4, :].bitcast(F32),
                                        ALU.subtract).then_inc(table_lo_set, 1)
            pool.wait_ge(v_set, NCH)

            def keep_near(b, par):
                nc.gpsimd.tensor_copy(v_near[:, par, :, :, :],
                                      vx[:, bass.ds(b * TPB, TPB), :, :]).then_inc(v_near_set, 1)

            keep_near(0, 0)
            keep_near(1, 1)

            def batch(b, par):
                pool.wait_ge(pv_ready, b * GROUPS + GROUPS)
                keep_near(b + 2, par)
                inv_std(b * 2 + NCH + 1, TPB)
                inv_std(b * 2 + NCH + 2, TPB)

            with pool.Fori(0, (B - 2) // 2) as i:
                batch(i * 2, 0)
                batch(i * 2 + 1, 1)
            for b in (B - 2, B - 1):
                inv_std(b * 2 + NCH + 1, TPB)
                inv_std(b * 2 + NCH + 2, TPB)

            with pool.Fori(0, NCH) as c:
                for k in range(0, NK, 2):
                    pool.wait_ge(g_hi_set, c * NK + (k + 1))
                    tok = bass.ds(c * CH, CH)
                    nc.gpsimd.tensor_tensor(g_parts[:, 1, k, tok], act_f[:, 0, k, :],
                                            g_parts[:, 0, k, tok].bitcast(F32), ALU.subtract).then_inc(g_lo_pool, 1)
            with pool.Fori(0, NCH) as c:
                inv_std(c + NCH + 2 * B + 1, TPC)

        @block.vector
        def _(dve):
            nc.vector.memset(pv[:, :], 0.0).then_inc(psum_zeroed, 1)

            held = [0]

            def hold(semaphore, value):
                dve.wait_ge(semaphore, value)
                if not isinstance(value, int):
                    held[0] += 1
                    nc.vector.memset(pad[0:1, held[0] % PADS:held[0] % PADS + 1], 0.0)

            def moments(src, tiles, base, at=0):
                for t in range(tiles):
                    last = nc.vector.bn_stats(stats[:, t, :], src(t))
                last.then_inc(dve_order, 1)
                hold(dve_order, base + 1)
                for t in range(tiles):
                    last = nc.vector.bn_aggr(mv[:, at + t, :], stats[:, t, :])
                last.then_inc(dve_order, 1)
                dve.wait_ge(dve_order, base + 2)
                var = mv[:, at:at + tiles, 1]
                nc.vector.tensor_scalar(var, var, EPS, None, ALU.add).then_inc(var_set, 1)

            def normalize(dst, src, t, at=0):
                return nc.vector.tensor_scalar(dst, src, mv[:, at + t, 0:1], rstd[:, at + t:at + t + 1],
                                               ALU.subtract, ALU.mult)

            def x_moments(c):
                dve.wait_ge(x_in[c], 16)
                moments(lambda t: xs[:, c * TPC + t, :], TPC, c * 2, c * TPC)

            def x_normalize(c):
                dve.wait_ge(rstd_set, c + 1)
                if c >= 2:
                    dve.wait_ge(xnT_ready, c - 1)
                for t in range(TPC):
                    last = normalize(x_norm[c % 2][:, t, :], xs[:, c * TPC + t, :], t, c * TPC)
                last.then_inc(xn_set, 1)

            x_moments(0)
            x_moments(1)
            x_normalize(0)
            x_moments(2)
            x_normalize(1)
            dve.wait_ge(qkv_w_in, 112)
            nc.vector.tensor_scalar(bq_sb[:, 0:1], bq_sb[:, 0:1], scale, None, ALU.mult).then_inc(bq_scaled, 1)
            x_moments(3)
            nc.vector.tensor_copy(identr[:, :], ident[:, :]).then_inc(identr_set, 1)
            for c in range(NCH):
                if c + 2 < NCH:
                    x_normalize(c + 2)
                dve.wait_ge(v_ready, c + 1)
                dve.wait_ge(const_set, 2)
                nc.vector.tensor_tensor(
                    vx[:, c * TPC:(c + 1) * TPC, :, 0:DK],
                    bank[3].rearrange("p (t h d) -> p t h d", t=TPC, h=H),
                    bv_bc[:, :].rearrange("p (o h d) -> p o h d", o=1, h=H).broadcast_to((P, TPC, H, DK)),
                    ALU.add).then_inc(v_set, 1)
                for i in range(2):
                    dve.wait_ge(qk_hi_set, c * 2 + (i + 1))
                    nc.vector.tensor_tensor(qk_lo[c][:, i, :], qk_f[:, c % 2, i, :],
                                            qk_hi[c][:, i, :].bitcast(F32), ALU.subtract).then_inc(qk_lo_set, 1)
            def maxima(b, s):
                for it in range(TPB):
                    hold(ms_ready, b * (2 * PAIRS) + (2 * s + it + 1))
                    for k in range(2):
                        h = 2 * s + k
                        col = P - it * P
                        last = nc.vector.tensor_tensor_reduce(
                            out=ms[it][:, k, :], in0=ms[it][:, k, :], in1=reverse(bias_max[:, h, WIN - S - col:WIN - col]), scale=1.0,
                            scalar=-3.4e38, op0=ALU.add, op1=ALU.max, accum_out=mx[:, it, h:h + 1])
                    last.then_inc(ms_read, 1)

            base = 2 * NCH

            def weigh(b, it):
                dve.wait_ge(o_ready, b * TPB + it + 1)
                heads = misc[:, :].rearrange("p (h c) -> p h c", h=H)
                n = b * 6 + base + 1 + it
                nc.vector.reciprocal(rsum[:, :], heads[:, :, DK]).then_inc(dve_order, 1)
                dve.wait_ge(dve_order, n)
                nc.vector.tensor_tensor(
                    on[:, it, :].rearrange("p (h d) -> p h d", h=H), heads[:, :, 0:DK],
                    rsum[:, :].rearrange("p (h o) -> p h o", o=1).broadcast_to((P, H, DK)),
                    ALU.mult).then_inc(on_set, 1)

            dve.wait_ge(out_w_in, 32)

            def attn_moments(b):
                dve.wait_ge(y_ready, b + 1)
                nc.vector.tensor_tensor(y[:, :, :], misc[:, 0:TPB * D].rearrange("p (t d) -> p t d", t=TPB),
                                        bo_bc[:, :].rearrange("p (o d) -> p o d", o=1).broadcast_to((P, TPB, D)),
                                        ALU.add).then_inc(y_read, 1)
                hold(y_read, b + 1)
                moments(lambda t: y[:, t, :], TPB, b * 6 + base + 2)

            def residual(b, tile):
                dve.wait_ge(rstd_set, b * 2 + NCH + 1)
                for t in range(TPB):
                    last = normalize(y[:, t, :], y[:, t, :], t)
                last.then_inc(y_norm, 1)
                dve.wait_ge(y_norm, b + 1)
                xb = xs[:, bass.ds(b * TPB, TPB), :] if not isinstance(b, int) else xs[:, TPB * b:TPB * b + TPB, :]
                nc.vector.tensor_tensor(xb, xb, y[:, :, :], ALU.add).then_inc(x1_set, 1)
                hold(x1_set, b + 1)
                moments(lambda t: xs[:, bass.ds(b * TPB + t, 1), :].rearrange("p o d -> p (o d)"), TPB,
                        b * 6 + base + 4)

            def second_norm(b):
                dve.wait_ge(rstd_set, b * 2 + NCH + 2)
                if not (isinstance(b, int) and b == 0):
                    dve.wait_ge(zT_ready, b)
                for t in range(TPB):
                    last = normalize(z[:, t, :], xs[:, bass.ds(b * TPB + t, 1), :].rearrange("p o d -> p (o d)"), t)
                last.then_inc(z_set, 1)

            def z_low(b):
                dve.wait_ge(z_hi_set, b + 1)
                tok = bass.ds(b * S, S)
                nc.vector.tensor_tensor(z_parts[:, 1, tok], misc[:, 0:S], z_parts[:, 0, tok].bitcast(F32),
                                        ALU.subtract).then_inc(z_lo_set, 1)

            def weights_low(piece):
                cols = slice(piece * WPIECE, (piece + 1) * WPIECE)
                dve.wait_ge(w_hi_set, piece + 1)
                nc.vector.tensor_tensor(w_lo[:, cols], w_lo[:, cols], w_hi[:, cols].bitcast(F32),
                                        ALU.subtract).then_inc(w_lo_set, 1)
                dve.wait_ge(w_lo_set, piece + 1)
                nc.vector.tensor_reduce(w_low_max[:, piece:piece + 1], w_lo[:, cols], AX.X, ALU.max,
                                        apply_absolute_value=True).then_inc(w_low_max_set, 1)

            for s in range(PAIRS):
                dve.wait_ge(max_bias_in[s // (PAIRS // 2)], 16)
                maxima(0, s)

            def batch(b, par, post=True, more=True):
                for s in range(PAIRS):
                    if not more:
                        for piece in PIECES_AT[s]:
                            weights_low(piece)
                    if post:
                        if s in (2, 3):
                            weigh(b - 1, s - 2)
                        if s == 5:
                            attn_moments(b - 1)
                        if s == 6:
                            residual(b - 1, None)
                    if more:
                        maxima(b + 1, s)
                    if post and s == 6:
                        second_norm(b - 1)
                    if post and s == 7:
                        z_low(b - 1)

            batch(0, 0, post=False)
            with dve.Fori(0, (B - 2) // 2) as i:
                batch(i * 2 + 1, 1)
                batch(i * 2 + 2, 0)
            batch(B - 1, 1, more=False)
            dve.wait_ge(w_low_max_set, WPIECES)
            nc.vector.tensor_reduce(w_low_top[:, :], w_low_max[:, :], AX.X, ALU.max).then_inc(w_low_top_set, 1)
            weigh(B - 1, 0)
            weigh(B - 1, 1)
            attn_moments(B - 1)
            residual(B - 1, None)
            second_norm(B - 1)

            z_low(B - 1)
            dve.wait_ge(w_low_row, 1)
            nc.vector.tensor_reduce(w_low_any[:, :], bank[0][0:1, 0:P], AX.X, ALU.max).then_inc(w_low_any_set, 1)

            dve.wait_ge(scales_in, 80)

            def gates(c, first=False):
                def low(k):
                    dve.wait_ge(g_hi_set, c * NK + (k + 1))
                    tok = bass.ds(c * CH, CH)
                    nc.vector.tensor_tensor(g_parts[:, 1, k, tok], act_f[:, 0, k, :],
                                            g_parts[:, 0, k, tok].bitcast(F32), ALU.subtract).then_inc(g_lo_dve, 1)

                for k in range(NK):
                    dve.wait_ge(silu_done, c * NK + (k + 1))
                    if not first:
                        if k % 2 == 0:
                            dve.wait_ge(g_lo_pool, c * (NK // 2) + (k // 2 - NK // 2 + 1))
                        else:
                            hold(g_lo_dve, c * (NK // 2) + (k // 2 - NK // 2 + 1))
                    nc.vector.scalar_tensor_tensor(
                        out=act_f[:, 0, k, :], in0=bank[2 * k + 1], scalar=hs[:, 1, k:k + 1],
                        in1=gate[:, k % 2, :], op0=ALU.mult, op1=ALU.mult).then_inc(gate_set, 1)
                    if k == 2:
                        low(1)
                low(3)

            gates(0, first=True)
            with dve.Fori(1, NCH) as c:
                gates(c)

            base3 = base + 6 * B

            def layer_low(c, i):
                for k in range(NK):
                    dve.wait_ge((a1_hi_set, a2_hi_set)[i], c * NK + (k + 1))
                    hi, lo = layer_parts(c, i, k)
                    nc.vector.tensor_tensor(lo, act_f[:, i, k, :], hi.bitcast(F32),
                                            ALU.subtract).then_inc((a1_lo_set, a2_lo_set)[i], 1)

            def last_norm(c):
                dve.wait_ge(y3_set, c + 1)
                moments(lambda t: xn[:, t, :], TPC, c * 2 + base3)
                dve.wait_ge(rstd_set, c + (NCH + 2 * B + 1))
                for t in range(TPC):
                    last = normalize(xn[:, t, :], xn[:, t, :], t)
                last.then_inc(y3_norm, 1)
                dve.wait_ge(y3_norm, c + 1)
                xc = xs[:, bass.ds(c * TPC, TPC), :]
                nc.vector.tensor_tensor(xc, xc, xn[:, :, :], ALU.add).then_inc(out_set, 1)

            layer_low(0, 0)
            layer_low(0, 1)
            with dve.Fori(1, NCH) as c:
                layer_low(c, 0)
                layer_low(c, 1)
                last_norm(c - 1)
            last_norm(NCH - 1)

        @block.scalar
        def _(act):
            for dst, src in ((bq_sb[:, 0:1], bq), (bq_sb[:, 1:2], bk), (bv_bc, bv.broadcast_to((P, D)))):
                act.dma_start(dst[:, :], src).then_inc(qkv_w_in, 16)
            for dst, src in ((wo_sb, wo), (bo_bc, bo.broadcast_to((P, D)))):
                act.dma_start(dst[:, :], src).then_inc(out_w_in, 16)
            act.wait_ge(qkv_w_in, 112)
            for g in range(2):
                load_table(act, g)

            def keep_xT(c):
                act.wait_ge(xnT_ready, c + 1)
                if c > 0:
                    act.wait_ge(v_ready, c)
                nc.scalar.copy(xT[:, :], bank[TBANK[c % 2]]).then_inc(xT_set, 1)

            def table_high(g):
                act.wait_ge(raw_in[g % 2], 16 * (g // 2 + 1))
                nc.scalar.copy(table[:, 0, 4 * g:4 * g + 4, :], reverse_rows(bias_raw[g][:, :, :])).then_inc(table_hi_set, 1)

            keep_xT(0)
            act.wait_ge(bq_scaled, 1)
            for c in range(NCH):
                if c >= 2:
                    act.wait_ge(qk_lo_set, (c - 1) * 2)
                for i, (ready, banks) in enumerate(((q_ready, QBANK), (k_ready, KBANK))):
                    act.wait_ge(ready, c + 1)
                    nc.scalar.activation(qk_f[:, c % 2, i, :], bank[banks[c % 2]], ACT.Identity,
                                         bias=bq_sb[:, i:i + 1], scale=scale if i == 0 else 1.0).then_inc(qk_f_set, 1)
                if c + 1 < NCH:
                    keep_xT(c + 1)
                for i in range(2):
                    act.wait_ge(qk_f_set, c * 2 + (i + 1))
                    nc.scalar.copy(qk_hi[c][:, i, :], qk_f[:, c % 2, i, :]).then_inc(qk_hi_set, 1)
                if c < 2:
                    table_high(c)
            for g in (2, 3):
                table_high(g)

            def minus_max(b, half):
                act.wait_ge(mT_ready, b * 2 + 1 + half)
                if not (isinstance(b, int) and b == 0):
                    act.wait_ge(mrow_in[half], b * 16)
                nc.scalar.mul(mrow[:, half, :], misc[0:HALF, 0:S], -1.0).then_inc(mrow_set, 1)

            def probabilities(b, s, first=False):
                act.wait_ge(st_ready, b * PAIRS + (s + 1))
                if not (first and s < PRING):
                    act.wait_ge(pv_ready, b * GROUPS + ((s - PRING) // 2 + 1))
                nc.scalar.activation(probs[:, s % PRING, :, :, :].rearrange("p k j n -> p (k j n)"),
                                     st[s % 2][:, :, :].rearrange("p k n -> p (k n)"), ACT.Exp).then_inc(exp_done, 1)

            def keep_weighted(b, par, g):
                act.wait_ge(pv_ready, b * GROUPS + (g + 1))
                nc.scalar.copy(oT[:, par, g, :], pv[:, 0:S]).then_inc(oT_set, 1)

            def keep_onT(b):
                act.wait_ge(onT_ready, b + 1)
                nc.scalar.copy(onT[:, :], misc[:, 0:S]).then_inc(onT_set, 1)

            def keep_zT(b):
                act.wait_ge(zT_ready, b + 1)
                nc.scalar.copy(z_parts[:, 0, bass.ds(b * S, S)], misc[:, 0:S]).then_inc(z_hi_set, 1)

            def weights_high(piece):
                act.wait_ge(ffn_w_in[matrix_of(piece)], 16)
                cols = slice(piece * WPIECE, (piece + 1) * WPIECE)
                nc.scalar.copy(w_hi[:, cols], w_lo[:, cols]).then_inc(w_hi_set, 1)

            minus_max(0, 0)
            act.wait_ge(table_lo_set, GROUPS - 1)

            def batch(b, par, first=False, more=True):
                for s in range(PAIRS):
                    if s == 1:
                        minus_max(b, 1)
                    if s == 4 and not first:
                        keep_onT(b - 1)
                    if s == 6 and more:
                        minus_max(b + 1, 0)
                    if not more:
                        for piece in PIECES_AT[s]:
                            weights_high(piece)
                    if s == 7 and not first:
                        keep_zT(b - 1)
                    probabilities(b, s, first)
                    if s == 0 and not first:
                        keep_weighted(b - 1, 1 - par, GROUPS - 1)
                    if first and s == 2:
                        act.wait_ge(table_lo_set, GROUPS)
                    if s >= 2 and s % 2 == 0:
                        keep_weighted(b, par, s // 2 - 1)

            batch(0, 0, first=True)
            with act.Fori(0, (B - 2) // 2) as i:
                batch(i * 2 + 1, 1)
                batch(i * 2 + 2, 0)
            batch(B - 1, 1, more=False)
            keep_weighted(B - 1, 1, GROUPS - 1)
            keep_onT(B - 1)
            keep_zT(B - 1)

            act.wait_ge(scales_in, 80)

            def gates(c, first=False):
                def high(k):
                    act.wait_ge(gate_set, c * NK + (k + 1))
                    nc.scalar.copy(g_parts[:, 0, k, bass.ds(c * CH, CH)], act_f[:, 0, k, :]).then_inc(g_hi_set, 1)

                for k in range(NK):
                    act.wait_ge(up_ready, c * NK + (k + 1))
                    if not (first and k < 2):
                        act.wait_ge(gate_set, c * NK + (k - 1))
                    nc.scalar.activation(gate[:, k % 2, :], bank[2 * k], ACT.Silu,
                                         scale=hs[:, 0, k:k + 1]).then_inc(silu_done, 1)
                    if k > 0:
                        high(k - 1)
                high(NK - 1)

            gates(0, first=True)
            with act.Fori(1, NCH) as c:
                gates(c)

            def layer(c, i, first=False):
                ready, done, hi_set, lo_set = ((a1_ready, a1_set, a1_hi_set, a1_lo_set),
                                               (a2_ready, a2_set, a2_hi_set, a2_lo_set))[i]
                for k in range(NK):
                    act.wait_ge(ready, c * NK + (k + 1))
                    if not first:
                        act.wait_ge(lo_set, c * NK + (k - NK + 1))
                    nc.scalar.activation(act_f[:, i, k, :], bank[HBANK[i][k]], ACT.Gelu,
                                         scale=hs[:, 2 + i, k:k + 1]).then_inc(done, 1)
                    act.wait_ge(done, c * NK + (k + 1))
                    nc.scalar.copy(layer_parts(c, i, k)[0], act_f[:, i, k, :]).then_inc(hi_set, 1)

            def keep_y3T(c):
                act.wait_ge(y3_ready, c + 1)
                nc.scalar.mul(y3T[:, :], bank[7], w3s_sb[:, 0:1]).then_inc(y3T_set, 1)

            def keep_y3(c, first=False):
                act.wait_ge(y3_back, c + 1)
                if not first:
                    act.wait_ge(out_set, c)
                nc.scalar.copy(xn[:, :, :].rearrange("p t d -> p (t d)"), bank[7]).then_inc(y3_set, 1)

            act.wait_ge(g_lo_pool, NCH * NK // 2)
            act.wait_ge(g_lo_dve, NCH * NK // 2)
            layer(0, 0, first=True)
            layer(0, 1, first=True)
            layer(1, 0)
            keep_y3T(0)
            layer(1, 1)
            keep_y3(0, first=True)
            with act.Fori(2, NCH) as c:
                layer(c, 0)
                keep_y3T(c - 1)
                layer(c, 1)
                keep_y3(c - 1)
            keep_y3T(NCH - 1)
            keep_y3(NCH - 1)

        @block.tensor
        def _(pe):
            mm = nc.tensor.matmul
            pe.wait_ge(qkv_w_in, 112)

            def x_T(c):
                pe.wait_ge(xn_set, c + 1)
                if c >= 2:
                    pe.wait_ge(xT_set, c - 1)
                for t in range(TPC):
                    last = nc.tensor.transpose(bank[TBANK[c % 2]][:, t * P:(t + 1) * P], x_norm[c % 2][:, t, :],
                                               ident[:, :])
                last.then_inc(xnT_ready, 1)

            x_T(0)
            for c in range(NCH):
                if c + 1 < NCH:
                    x_T(c + 1)
                pe.wait_ge(xT_set, c + 1)
                if c >= 2:
                    pe.wait_ge(qk_f_set, (c - 1) * 2)
                mm(bank[QBANK[c % 2]], wq_sb[:, :], xT[:, :], start=True, stop=True).then_inc(q_ready, 1)
                mm(bank[KBANK[c % 2]], wk_sb[:, :], xT[:, :], start=True, stop=True).then_inc(k_ready, 1)
                if c > 0:
                    pe.wait_ge(v_set, c)
                for t in range(TPC):
                    last = mm(bank[3][:, t * P:(t + 1) * P], xT[:, t * P:(t + 1) * P], wv_sb[:, :],
                              start=True, stop=True)
                last.then_inc(v_ready, 1)

            def rows(r, par, h, extra):
                r0 = 64 * (h // HALF)
                return r[r0:r0 + KROWS + extra, par, h % HALF, :]

            def max_scores(b, par, s, first=False):
                if s % (PAIRS // 2) == 0:
                    pe.wait_ge(rows_in[s // (PAIRS // 2)][par], b * (ROW_DMAS * 8) + ROW_DMAS * (16 - 8 * par))
                for it in range(TPB):
                    if not (first and s == 0):
                        pe.wait_ge(ms_read, b * (2 * PAIRS) + (2 * s + it - 1))
                    for k in range(2):
                        h = 2 * s + k
                        last = mm(ms[it][:, k, :], rows(q_rows, par, h, 0)[:, it * P:(it + 1) * P],
                                  rows(k_rows, par, h, 0), start=True, stop=True)
                    last.then_inc(ms_ready, 1)

            def maxima_T(b, half):
                pe.wait_ge(ms_read, b * (2 * PAIRS) + PAIRS * (half + 1))
                for it in range(TPB):
                    last = mm(misc[0:HALF, it * P:(it + 1) * P], mx[:, it, half * HALF:(half + 1) * HALF],
                              ident[:, :], start=True, stop=True)
                last.then_inc(mT_ready, 1)

            def scores(b, par, s, first=False):
                if s % (PAIRS // 2) == 0:
                    pe.wait_ge(mrow_in[s // (PAIRS // 2)], b * 16 + 16)
                if not (first and s < 2):
                    pe.wait_ge(exp_done, b * PAIRS + (s - 1))
                if first:
                    pe.wait_ge(table_lo_set, s // 2 + 1)
                for k in range(2):
                    for a in range(2):
                        mm(st[s % 2][:, k, :], identr[:, :], windows(table[:, a, 2 * s + k, :], 0, P, 2, S),
                           start=(a == 0), stop=False)
                for k in range(2):
                    h = 2 * s + k
                    for j, jt in enumerate((1, 0)):
                        last = mm(st[s % 2][:, k, j * S:(j + 1) * S], rows(k_rows, par, h, 1)[:, jt * P:(jt + 1) * P],
                                  rows(q_rows, par, h, 1), start=False, stop=(j == 1))
                last.then_inc(st_ready, 1)

            def weighted(b, par, g, first=False):
                pe.wait_ge(exp_done, b * PAIRS + (2 * g + 2))
                if g == 0:
                    pe.wait_ge(v_near_set, b + 1)
                if not (first and g == 0):
                    pe.wait_ge(oT_set, b * GROUPS + g)
                for j, jt in enumerate((1, 0)):
                    for r in range(4):
                        h = 4 * g + r
                        last = mm(pv[32 * r:32 * r + VC, 0:S], v_near[:, par, jt, h, :],
                                  probs[:, (2 * g + r // 2) % PRING, r % 2, j, :], start=(j == 0), stop=(j == 1))
                last.then_inc(pv_ready, 1)

            def back(b, par, it):
                if it == 0:
                    pe.wait_ge(oT_set, b * GROUPS + GROUPS)
                else:
                    pe.wait_ge(on_set, b * TPB + it)
                for g in range(GROUPS):
                    last = nc.tensor.transpose(misc[:, g * P:(g + 1) * P], oT[:, par, g, it * P:(it + 1) * P],
                                               ident[:, :])
                last.then_inc(o_ready, 1)

            def heads_T(b):
                pe.wait_ge(on_set, b * TPB + TPB)
                for it in range(TPB):
                    last = nc.tensor.transpose(misc[:, it * P:(it + 1) * P], on[:, it, :], ident[:, :])
                last.then_inc(onT_ready, 1)

            def project(b):
                pe.wait_ge(onT_set, b + 1)
                for it in range(TPB):
                    last = mm(misc[:, it * P:(it + 1) * P], onT[:, it * P:(it + 1) * P], wo_sb[:, :],
                              start=True, stop=True)
                last.then_inc(y_ready, 1)

            def norm_T(b):
                pe.wait_ge(z_set, b + 1)
                for it in range(TPB):
                    last = nc.tensor.transpose(misc[:, it * P:(it + 1) * P], z[:, it, :], ident[:, :])
                last.then_inc(zT_ready, 1)

            pe.wait_ge(qk_f_set, 2 * NCH)
            pe.wait_ge(v_set, NCH)
            for s in range(PAIRS):
                if s == 6:
                    maxima_T(0, 0)
                max_scores(0, 0, s, first=True)
            pe.wait_ge(identr_set, 1)
            pe.wait_ge(ones_set, 2)
            pe.wait_ge(out_w_in, 32)
            pe.wait_ge(psum_zeroed, 1)

            def batch(b, par, first=False, more=True):
                for s in range(PAIRS):
                    if more:
                        max_scores(b + 1, 1 - par, s)
                    if s == 1:
                        if not more:
                            pe.wait_ge(z_lo_set, b - 1)
                        if first:
                            pe.wait_ge(mrow_set, 1)
                        else:
                            pe.wait_ge(oT_set, b * GROUPS)
                        maxima_T(b, 1)
                    if s == 7 and not first:
                        if more:
                            pe.wait_ge(mrow_set, b * 2 + 3)
                        else:
                            pe.wait_ge(y_read, b)
                        norm_T(b - 1)
                    scores(b, par, s, first)
                    if s == 0 and not first:
                        weighted(b - 1, 1 - par, GROUPS - 1)
                    if s >= 2 and s % 2 == 0:
                        weighted(b, par, s // 2 - 1, first)
                    if s == 1 and not first:
                        pe.wait_ge(mrow_set, b * 2 + 2)
                        back(b - 1, 1 - par, 0)
                    if s == 2 and not first:
                        back(b - 1, 1 - par, 1)
                    if s == 3 and not first:
                        heads_T(b - 1)
                    if s == 4 and not first:
                        project(b - 1)
                    if s == 5 and more:
                        if first:
                            pe.wait_ge(mrow_set, 2)
                        else:
                            pe.wait_ge(y_read, b)
                        maxima_T(b + 1, 0)

            batch(0, 0, first=True)
            with pe.Fori(0, (B - 2) // 2) as i:
                batch(i * 2 + 1, 1)
                batch(i * 2 + 2, 0)
            batch(B - 1, 1, more=False)
            weighted(B - 1, 1, GROUPS - 1)
            pe.wait_ge(z_lo_set, B - 1)
            back(B - 1, 1, 0)
            back(B - 1, 1, 1)
            heads_T(B - 1)
            project(B - 1)
            pe.wait_ge(y_read, B)
            norm_T(B - 1)
            pe.wait_ge(w_low_top_set, 1)
            pe.wait_ge(exp_done, B * PAIRS)
            mm(bank[0][0:1, 0:P], w_low_top[:, :], ident[:, :], start=True, stop=True).then_inc(w_low_row, 1)

            def product(o, weight, x, exact, first=True, last=True):
                hi, lo = x
                w = w_hi[:, weight]
                mm(o, w, hi, start=first, stop=False)
                done = mm(o, w, lo, start=False, stop=last and exact)
                if not exact:
                    mm(o, w_lo[:, weight], hi.bitcast(F32), start=False, stop=False)
                    done = mm(o, w_lo[:, weight], lo.bitcast(F32), start=False, stop=last)
                return done

            def columns(at, j, k, width):
                return slice(at + j * width + k * P, at + j * width + (k + 1) * P)

            def gates(c, exact, first=False):
                zc = [z_parts[:, a, bass.ds(c * CH, CH)] for a in range(2)]
                for k in range(NK):
                    if not first:
                        pe.wait_ge(gate_set, c * NK + (k - NK + 1))
                    product(bank[2 * k], columns(W1, 0, k, HID), zc, exact)
                    product(bank[2 * k + 1], columns(W2, 0, k, HID), zc, exact).then_inc(up_ready, 1)

            def layer1(c, exact, first=False):
                for k in range(NK):
                    if not first:
                        if k < 3:
                            pe.wait_ge(a1_set, c * NK + (k - NK + 1))
                        else:
                            pe.wait_ge(a2_set, c * NK)
                    for j in range(NK):
                        last = product(bank[HBANK[0][k]], columns(W_H1, j, k, HID), layer_parts(c, 1, j), exact,
                                       first=(j == 0), last=(j == NK - 1))
                    last.then_inc(a1_ready, 1)

            def layer2(c, exact, first=False):
                for k in range(NK):
                    if not first and k < 3:
                        pe.wait_ge(a2_set, c * NK + (k - NK + 1))
                    for j in range(NK):
                        if k == 0:
                            pe.wait_ge(a1_lo_set, c * NK + (j + 1))
                        last = product(bank[HBANK[1][k]], columns(W_H2, j, k, HID), layer_parts(c, 0, j), exact,
                                       first=(j == 0), last=(j == NK - 1))
                    last.then_inc(a2_ready, 1)

            def layer3(c, exact, first=False):
                if not first:
                    pe.wait_ge(y3_set, c)
                for j in range(NK):
                    pe.wait_ge(a2_lo_set, c * NK + (j + 1))
                    last = product(bank[7], columns(W3, j, 0, D), layer_parts(c, 1, j), exact,
                                       first=(j == 0), last=(j == NK - 1))
                last.then_inc(y3_ready, 1)

            def tokens_back(c):
                pe.wait_ge(y3T_set, c + 1)
                for t in range(TPC):
                    last = nc.tensor.transpose(bank[7][:, t * P:(t + 1) * P], y3T[:, t * P:(t + 1) * P], ident[:, :])
                last.then_inc(y3_back, 1)

            def ffn(exact):
                gates(0, exact, first=True)
                with pe.Fori(1, NCH) as c:
                    gates(c, exact)
                pe.wait_ge(gate_set, NCH * NK)
                pe.wait_ge(g_hi_set, NCH * NK)
                pe.wait_ge(g_lo_pool, NCH * NK // 2)
                pe.wait_ge(g_lo_dve, NCH * NK // 2)
                layer1(0, exact, first=True)
                layer2(0, exact, first=True)
                layer1(1, exact)
                layer3(0, exact, first=True)
                layer2(1, exact)
                tokens_back(0)
                with pe.Fori(2, NCH) as c:
                    layer1(c, exact)
                    layer3(c - 1, exact)
                    layer2(c, exact)
                    tokens_back(c - 1)
                layer3(NCH - 1, exact)
                tokens_back(NCH - 1)

            pe.wait_ge(w_hi_set, WPIECES)
            pe.wait_ge(ms_read, B * 2 * PAIRS)
            pe.wait_ge(oT_set, B * GROUPS)
            pe.wait_ge(z_hi_set, B)
            pe.wait_ge(z_lo_set, B)
            pe.wait_ge(w_low_any_set, 1)
            some_low = pe.value_load(w_low_any[0:1, 0:1].bitcast(I32))
            with pe.If(some_low != 0):
                ffn(exact=False)
            with pe.Else():
                ffn(exact=True)

    return nc


def kernel(**inputs):
    import numpy as np
    import concourse.bacc as bacc
    from concourse.bass_utils import run_bass_kernel_spmd

    a = {k.removeprefix("L0_"): np.asarray(v) for k, v in inputs.items()}
    w = a["attn_W_qkv"]
    bqkv = a["attn_b_qkv"]
    rel = np.ascontiguousarray(a["attn_rel_bias"].T)
    pad = ((0, 0), (P - 1, EXT - REL - (P - 1)))
    col = lambda v: v.reshape(-1, 1)
    by_dim = lambda m: m.reshape(-1, H, DK).transpose(0, 2, 1).reshape(-1, D)
    tiles = lambda v: v.reshape(NK, P).T
    weights = lambda m: m.T.reshape(NK, P, -1).transpose(1, 0, 2).reshape(P, -1)
    arrays = {
        "x": a["attn_x"].reshape(TOK, D),
        "wq": by_dim(w[:, 0:D]), "wk": by_dim(w[:, D:2 * D]), "wv": w[:, 2 * D:3 * D],
        "bq": by_dim(bqkv[None, 0:D]).T, "bk": by_dim(bqkv[None, D:2 * D]).T, "bv": bqkv[None, 2 * D:3 * D],
        "wo": a["attn_W_out"], "bo": a["attn_b_out"][None, :],
        "ext": np.pad(rel, pad, mode="edge")[:, ::-1], "ext_max": np.pad(rel[:, ::-1], pad, mode="edge")[:, ::-1],
        "w1": a["ffn_w1_w"].T, "s1": tiles(a["ffn_w1_s"]), "w2": a["ffn_w2_w"].T, "s2": tiles(a["ffn_w2_s"]),
        "h1": weights(a["ffn_h1_w"]), "h1s": tiles(a["ffn_h1_s"]),
        "h2": weights(a["ffn_h2_w"]), "h2s": tiles(a["ffn_h2_s"]),
        "w3": weights(a["ffn_w3_w"]), "w3s": col(a["ffn_w3_s"]),
        "ident_in": np.eye(P, dtype=np.float32),
    }
    arrays = {k: np.ascontiguousarray(v) for k, v in arrays.items()}
    nc = bacc.Bacc("TRN2", target_bir_lowering=False, num_devices=1)
    args = [nc.dram_tensor(k, v.shape, mybir.dt.from_np(v.dtype), kind="ExternalInput").ap() for k, v in arrays.items()]
    out = nc.dram_tensor("out", (TOK, D), F32, kind="ExternalOutput").ap()
    build(nc, *args, out)
    r = run_bass_kernel_spmd(nc, [arrays], core_ids=[0])
    return r.results[0]["out"].reshape(B, S, D)
```

```python
import concourse.bass as bass
from concourse import mybir
from contextlib import ExitStack

F32 = mybir.dt.float32
F32R = mybir.dt.float32r
I32 = mybir.dt.int32
AX = mybir.AxisListType
ALU = mybir.AluOpType
ACT = mybir.ActivationFunctionType

B, S, D = 8, 256, 128
H, DK = 16, 8
HID = 512
P = 128
EPS = 1e-5
TOK = B * S
NT = TOK // P
TPB = S // P
MAX_REL = 128
REL = 2 * MAX_REL + 1
WIN = P + S
EXT = WIN + P - 1
CH = 512
NCH = TOK // CH
TPC = CH // P
NK = HID // P
PAIRS = H // 2
GROUPS = H // 4
HALF = H // 2
PARTS = 4
KROWS = PARTS * DK
VC = DK + 1
PADS = 128
ADDED = (0, 2)
PRING = 4
W1, W2, W_H1, W_H2, W3 = 0, HID, 2 * HID, 2 * HID + NK * HID, 2 * HID + 2 * NK * HID
WCOLS = W3 + NK * D
WPIECE = 512


def windows(ap, start, step, count, width):
    return bass.AP(tensor=ap.tensor, offset=ap.offset + start, ap=[list(ap.ap[0]), [step, count], [1, width]])


def reverse(ap):
    n = ap.shape[-1]
    return bass.AP(tensor=ap.tensor, offset=ap.offset + n - 1, ap=[list(ap.ap[0]), [-1, n]])


def reverse_rows(ap):
    (row, m), (_, n) = ap.ap[1], ap.ap[2]
    return bass.AP(tensor=ap.tensor, offset=ap.offset + n - 1, ap=[list(ap.ap[0]), [row, m], [-1, n]])


def build(nc, x, wq, wk, wv, bq, bk, bv, wo, bo, ext, ext_max, w1, s1, w2, s2, h1, h1s, h2, h2s, w3, w3s,
          ident_in, out):
    ctx = ExitStack()
    with ctx:
        def sb(name, shape, dt=F32):
            return ctx.enter_context(nc.sbuf_tensor(name, shape, dt))

        def sem(name):
            return ctx.enter_context(nc.semaphore(name))

        ident = sb("ident", [P, P])
        identr = sb("identr", [P, P], F32R)
        wq_sb = sb("wq_sb", [P, D])
        wk_sb = sb("wk_sb", [P, D])
        wv_sb = sb("wv_sb", [P, D])
        wo_sb = sb("wo_sb", [P, D])
        bq_sb = sb("bq_sb", [P, 2])
        bv_bc = sb("bv_bc", [P, D])
        bo_bc = sb("bo_bc", [P, D])
        xs = sb("xs", [P, NT, D])
        stats = sb("stats", [P, TPC, 6])
        mv = sb("mv", [P, NT, 2])
        rstd = sb("rstd", [P, NT])
        mhalf = sb("mhalf", [P, TPC])
        table_loaded = sb("table_loaded", [P, 1])
        xn = sb("xn", [P, TPC, D])
        xT = sb("xT", [P, CH])
        z_parts = sb("z_parts", [P, 2, TOK], F32R)
        w_hi = sb("w_hi", [P, WCOLS], F32R)
        qk_parts = [view[:, 2 * CH * n:2 * CH * (n + 2)].rearrange("p (a i n) -> p a i n", a=2, i=2)
                    for view in (z_parts[:, :, :].rearrange("p a n -> p (a n)"), w_hi) for n in (0, 2)]
        qk_hi = [parts[:, 0, :, :] for parts in qk_parts]
        qk_lo = [parts[:, 1, :, :] for parts in qk_parts]
        room = sb("room", [P, 2 * NK * (TOK + CH)], F32R)
        table = room[:, 0:2 * H * WIN].rearrange("p (a h c) -> p a h c", a=2, h=H)
        rows_at = 2 * H * WIN
        q_rows = room[:, rows_at:rows_at + 2 * HALF * S].rearrange("p (a h n) -> p a h n", a=2, h=HALF)
        k_rows = room[:, rows_at + 2 * HALF * S:rows_at + 4 * HALF * S].rearrange("p (a h n) -> p a h n", a=2, h=HALF)
        g_parts = room[:, 0:2 * NK * TOK].rearrange("p (a k n) -> p a k n", a=2, k=NK)
        a1_parts = room[:, 2 * NK * TOK:2 * NK * (TOK + CH)].rearrange("p (a k n) -> p a k n", a=2, k=NK)
        vx = sb("vx", [P, NT, H, VC])
        v_near = sb("v_near", [P, 2, TPB, H, VC])
        big = sb("big", [P, NK * TOK])
        bias_max = big[:, 0:H * WIN].rearrange("p (h c) -> p h c", h=H)
        pad = sb("pad", [P, PADS])
        mx = sb("mx", [P, TPB, H])
        mrow = sb("mrow", [HALF, 2, S], F32R)
        ring = sb("ring", [P, PRING * 4 * S])
        probs = ring[:, :].rearrange("p (a k j n) -> p a k j n", a=PRING, k=2, j=2)
        bias_raw = [place[:, at:at + 4 * WIN].rearrange("p (h c) -> p h c", h=4)
                    for place, at in ((ring, 0), (ring, 4 * WIN), (ring, 0), (big, H * WIN))]
        bias_added = sb("bias_added", [P, len(ADDED), 2, WIN])
        oT = big[:, H * WIN:H * WIN + 2 * GROUPS * S].rearrange(
            "p (a g n) -> p a g n", a=2, g=GROUPS)
        qk_f = big[:, H * WIN:H * WIN + 4 * CH].rearrange("p (a i n) -> p a i n", a=2, i=2)
        rsum = sb("rsum", [P, H])
        on = sb("on", [P, TPB, D])
        onT = sb("onT", [P, S])
        y_and_z = sb("y_and_z", [P, 2 * TPB * D])
        y = y_and_z[:, 0:TPB * D].rearrange("p (t d) -> p t d", t=TPB)
        z = y_and_z[:, TPB * D:2 * TPB * D].rearrange("p (t d) -> p t d", t=TPB)
        w_lo = big[:, 0:WCOLS]
        w_low_max = sb("w_low_max", [P, WCOLS // WPIECE])
        w_low_top = sb("w_low_top", [P, 1])
        w_low_any = sb("w_low_any", [1, 1])
        hs = sb("hs", [P, 4, NK])
        w3s_sb = sb("w3s_sb", [P, 1])
        act_f = ring[:, 0:2 * NK * CH].rearrange("p (a k n) -> p a k n", a=2, k=NK)
        gate = bias_added[:, :, :, :].rearrange("p i k c -> p (i k c)")[:, 0:2 * CH].rearrange(
            "p (a n) -> p a n", a=2)
        y3T = y_and_z[:, 0:CH]

        x_norm = (xn, y_and_z[:, :].rearrange("p (t d) -> p t d", t=TPC))

        st = [ctx.enter_context(nc.psum_tensor(f"st{i}", [P, 2, 2 * S], F32)) for i in range(2)]
        ms = [ctx.enter_context(nc.psum_tensor(f"ms{i}", [P, 2, S], F32)) for i in range(2)]
        pv = ctx.enter_context(nc.psum_tensor("pv", [P, 512], F32))
        misc = ctx.enter_context(nc.psum_tensor("misc", [P, 512], F32))
        ms_first = ms + [st[0][:, i, :].rearrange("p (k n) -> p k n", k=2) for i in range(2)]
        bank = [st[0][:, 0, :], st[0][:, 1, :], st[1][:, 0, :], st[1][:, 1, :],
                ms[0][:, :, :].rearrange("p a n -> p (a n)"), ms[1][:, :, :].rearrange("p a n -> p (a n)"),
                pv[:, :], misc[:, :]]

        TBANK, QBANK, KBANK = (0, 4), (1, 5), (2, 7)
        GBANK = ((0, 1), (2, 3))
        HBANK = ((4, 5, 6, 4), (5, 6, 4, 5))

        q_dram = nc.dram_tensor("q_parts", (2, P, TOK), F32, kind="Internal").ap()
        k_dram = nc.dram_tensor("k_parts", (3, P, TOK), F32, kind="Internal").ap()

        x_in = [sem(f"x_in{c}") for c in range(NCH)]
        qkv_w_in = sem("qkv_w_in")
        out_w_in = sem("out_w_in")
        max_bias_in = [sem(f"max_bias_in{i}") for i in range(2)]
        raw_in = [sem(f"raw_in{i}") for i in range(2)]
        scales_in = sem("scales_in")
        ffn_w_in = [sem(f"ffn_w_in{i}") for i in range(5)]
        const_set = sem("const_set")
        psum_zeroed = sem("psum_zeroed")
        bq_scaled = sem("bq_scaled")
        identr_set = sem("identr_set")
        ones_set = sem("ones_set")
        table_hi_set = sem("table_hi_set")
        table_lo_set = sem("table_lo_set")
        dve_order = sem("dve_order")
        var_set = sem("var_set")
        rstd_set = sem("rstd_set")
        xn_set = sem("xn_set")
        xnT_ready = sem("xnT_ready")
        xT_set = sem("xT_set")
        q_ready = sem("q_ready")
        k_ready = sem("k_ready")
        v_ready = sem("v_ready")
        qk_f_set = sem("qk_f_set")
        qk_hi_set = sem("qk_hi_set")
        qk_lo_set = sem("qk_lo_set")
        v_set = sem("v_set")
        parts_out = [sem(f"parts_out{i}") for i in range(2)]
        rows_in = [[sem(f"rows_in{i}{p}") for p in range(2)] for i in range(2)]
        mrow_in = [sem(f"mrow_in{i}") for i in range(2)]
        ms_ready = sem("ms_ready")
        ms_read = sem("ms_read")
        mT_ready = sem("mT_ready")
        mrow_set = sem("mrow_set")
        st_ready = sem("st_ready")
        added_in = sem("added_in")
        added_set = sem("added_set")
        exp_done = sem("exp_done")
        pv_ready = sem("pv_ready")
        oT_set = sem("oT_set")
        o_ready = sem("o_ready")
        on_set = sem("on_set")
        onT_ready = sem("onT_ready")
        onT_set = sem("onT_set")
        y_ready = sem("y_ready")
        y_read = sem("y_read")
        y_norm = sem("y_norm")
        x1_set = sem("x1_set")
        v_near_set = sem("v_near_set")
        z_set = sem("z_set")
        zT_ready = sem("zT_ready")
        z_hi_set = sem("z_hi_set")
        z_lo_set = sem("z_lo_set")
        w_hi_set = sem("w_hi_set")
        w_lo_set = sem("w_lo_set")
        w_lo_dve = sem("w_lo_dve")
        w_low_max_set = sem("w_low_max_set")
        w_low_top_set = sem("w_low_top_set")
        w_low_row = sem("w_low_row")
        w_low_any_set = sem("w_low_any_set")
        up_ready = sem("up_ready")
        silu_done = sem("silu_done")
        gate_set = sem("gate_set")
        g_hi_act = sem("g_hi_act")
        g_lo_pool = sem("g_lo_pool")
        g_hi_dve = sem("g_hi_dve")
        g_lo_dve = sem("g_lo_dve")
        a1_ready = sem("a1_ready")
        a1_set = sem("a1_set")
        a1_hi_set = sem("a1_hi_set")
        a1_lo_set = sem("a1_lo_set")
        a2_ready = sem("a2_ready")
        a2_set = sem("a2_set")
        a2_hi_set = sem("a2_hi_set")
        a2_lo_set = sem("a2_lo_set")
        y3_ready = sem("y3_ready")
        y3T_set = sem("y3T_set")
        y3_back = sem("y3_back")
        y3_set = sem("y3_set")
        y3_norm = sem("y3_norm")
        out_set = sem("out_set")
        out_done = sem("out_done")

        block = ctx.enter_context(nc.Block())

        def layer_parts(c, i, k):
            if i == 0:
                return a1_parts[:, 0, k, :], a1_parts[:, 1, k, :]
            tok = bass.ds(c * CH, CH)
            return g_parts[:, 0, k, tok], g_parts[:, 1, k, tok]

        ROW_DMAS = PARTS
        PARTS_OUT = 5 * 16

        def load_table(eng, g):
            eng.dma_start(bias_raw[g][:, :, :],
                          bass.AP(tensor=ext.tensor, offset=4 * g * EXT,
                                  ap=[[1, P], [EXT, 4], [1, WIN]])).then_inc(raw_in[g % 2], 16)

        scale = float(1.0 / DK ** 0.5)

        def matrix_of(piece):
            return sum(piece * WPIECE >= at for at in (W2, W_H1, W_H2, W3))

        WPIECES = WCOLS // WPIECE
        HIGH_AT = ((0, 1, 2), (3, 4), (5, 6), (7, 8), (9, 10), (), (), ())
        LOW_AT = ((), (0,), (1,), (2, 3), (7, 4), (8, 5), (9, 6), (10,))
        POOL_PIECES = 7
        GPLACE = (0, 1, 1, 0)

        @block.sync
        def _(sp):
            xv = x.rearrange("(t p) d -> p t d", p=P)
            for c, (dst, src) in enumerate(((ident, ident_in), (wq_sb, wq), (wk_sb, wk), (wv_sb, wv))):
                sp.dma_start(xs[:, c * TPC:(c + 1) * TPC, :], xv[:, c * TPC:(c + 1) * TPC, :]).then_inc(x_in[c], 16)
                sp.dma_start(dst[:, :], src).then_inc(qkv_w_in, 16)
            def load_bias_max(half):
                sp.dma_start(bias_max[:, HALF * half:HALF * (half + 1), :],
                             bass.AP(tensor=ext_max.tensor, offset=HALF * half * EXT,
                                     ap=[[1, P], [EXT, HALF], [1, WIN]])).then_inc(max_bias_in[half], 16)

            load_bias_max(0)

            def store_parts(c):
                tok = slice(c * CH, (c + 1) * CH)
                sp.wait_ge(qk_hi_set, c * 2 + 2)
                sp.dma_start(q_dram[0, :, tok], qk_hi[c][:, 0, :].bitcast(F32)).then_inc(parts_out[c > 0], 16)
                for plane in (0, 2):
                    sp.dma_start(k_dram[plane, :, tok], qk_hi[c][:, 1, :].bitcast(F32)).then_inc(parts_out[c > 0], 16)
                sp.wait_ge(qk_lo_set, c * 2 + 2)
                sp.dma_start(q_dram[1, :, tok], qk_lo[c][:, 0, :].bitcast(F32)).then_inc(parts_out[c > 0], 16)
                sp.dma_start(k_dram[1, :, tok], qk_lo[c][:, 1, :].bitcast(F32)).then_inc(parts_out[c > 0], 16)

            def load_rows(b, par, half):
                for c in range(0, PARTS, 2):
                    r = 2 * 32 * half + DK * c
                    for rows, dram, part in ((q_rows, q_dram, 0), (k_rows, k_dram, c // 2)):
                        src = bass.AP(tensor=dram.tensor, offset=(part * P + half * HALF) * TOK + b * S,
                                      ap=[[H * TOK, 2 * DK], [TOK, HALF], [1, S]])
                        sp.dma_start(rows[r:r + 2 * DK, par, :, :].bitcast(F32), src).then_inc(rows_in[half][par], 16)

            def load_mrow(b, par, half):
                sp.wait_ge(mrow_set, b * 2 + 1 + half)
                r = 64 * half + KROWS
                sp.dma_start(q_rows[r:r + 1, par, :, :].bitcast(F32), mrow[:, half, :].bitcast(F32)).then_inc(mrow_in[half], 16)

            store_parts(0)
            sp.wait_ge(parts_out[0], PARTS_OUT)
            for half in range(2):
                load_rows(0, 0, half)
            load_bias_max(1)
            sp.wait_ge(table_lo_set, 1)
            load_table(sp, 2)
            for half in range(2):
                load_rows(1, 1, half)
            sp.wait_ge(qk_hi_set, NCH * 2)
            sp.wait_ge(qk_lo_set, NCH * 2)
            load_table(sp, 3)
            load_mrow(0, 0, 0)
            for i, s in enumerate(ADDED):
                sp.dma_start(bias_added[:, i, :, :], bass.AP(tensor=ext.tensor, offset=2 * s * EXT,
                                                             ap=[[1, P], [EXT, 2], [1, WIN]])).then_inc(added_in, 16)
            store_parts(1)
            for c in range(2, NCH):
                store_parts(c)
            for dst, src in ((hs[:, 0, :], s1), (hs[:, 1, :], s2), (hs[:, 2, :], h1s), (hs[:, 3, :], h2s),
                             (w3s_sb[:, :], w3s)):
                sp.dma_start(dst, src).then_inc(scales_in, 16)

            def batch(b, par, more=True, ahead=True):
                load_mrow(b, par, 1)
                if ahead:
                    sp.wait_ge(st_ready, b * PAIRS + PAIRS // 2)
                    sp.wait_ge(parts_out[1], (NCH - 1) * PARTS_OUT)
                    load_rows(b + 2, par, 0)
                if more:
                    load_mrow(b + 1, 1 - par, 0)
                if ahead:
                    sp.wait_ge(st_ready, b * PAIRS + PAIRS)
                    load_rows(b + 2, par, 1)

            with sp.Fori(0, (B - 2) // 2) as i:
                batch(i * 2, 0)
                batch(i * 2 + 1, 1)
            batch(B - 2, 0, ahead=False)
            matrices = ((W1, w1), (W2, w2), (W_H1, h1), (W_H2, h2), (W3, w3))

            def load_weights(which):
                for i in which:
                    at, src = matrices[i]
                    sp.dma_start(w_lo[:, at:at + src.shape[-1]], src).then_inc(ffn_w_in[i], 16)

            sp.wait_ge(ms_read, (B - 1) * 2 * PAIRS + PAIRS)
            load_weights((0, 1, 2))
            sp.wait_ge(ms_read, B * 2 * PAIRS)
            load_weights((3, 4))
            batch(B - 1, 1, more=False, ahead=False)
            ov = out.rearrange("(t p) d -> p t d", p=P)
            with sp.Fori(0, NCH) as c:
                sp.wait_ge(out_set, c + 1)
                sp.dma_start(ov[:, bass.ds(c * TPC, TPC), :], xs[:, bass.ds(c * TPC, TPC), :]).then_inc(out_done, 16)
            sp.wait_ge(out_done, NCH * 16)

        @block.gpsimd
        def _(pool):
            nc.gpsimd.memset(mhalf[:, :], -0.5).then_inc(const_set, 1)
            pool.wait_ge(const_set, 1)

            def inv_std(n, width, at=0):
                pool.wait_ge(var_set, n)
                nc.gpsimd.tensor_tensor(rstd[:, at:at + width], mv[:, at:at + width, 1], mhalf[:, 0:width],
                                        ALU.pow).then_inc(rstd_set, 1)

            for c in range(NCH):
                inv_std(c + 1, TPC, c * TPC)
                if c == 0:
                    nc.gpsimd.memset(vx[:, :, :, DK:VC], 1.0).then_inc(const_set, 1)
            pool.wait_ge(rstd_set, NCH)
            nc.gpsimd.memset(k_rows[KROWS:KROWS + 1, :, :, :].bitcast(F32), 1.0).then_inc(ones_set, 1)
            pool.wait_ge(ones_set, 1)
            r = 64 + KROWS
            nc.gpsimd.memset(k_rows[r:r + 1, :, :, :].bitcast(F32), 1.0).then_inc(ones_set, 1)
            pool.wait_ge(ones_set, 2)
            for g in range(GROUPS):
                pool.wait_ge(table_hi_set, g + 1)
                nc.gpsimd.tensor_tensor(table[:, 1, 4 * g:4 * g + 4, :], reverse_rows(bias_raw[g][:, :, :]),
                                        table[:, 0, 4 * g:4 * g + 4, :].bitcast(F32),
                                        ALU.subtract).then_inc(table_lo_set, 1)
            pool.wait_ge(v_set, NCH)

            def keep_near(b, par):
                nc.gpsimd.tensor_copy(v_near[:, par, :, :, :],
                                      vx[:, bass.ds(b * TPB, TPB), :, :]).then_inc(v_near_set, 1)

            keep_near(0, 0)
            keep_near(1, 1)

            def batch(b, par):
                pool.wait_ge(pv_ready, b * GROUPS + GROUPS)
                keep_near(b + 2, par)
                inv_std(b * 2 + NCH + 1, TPB)
                inv_std(b * 2 + NCH + 2, TPB)

            with pool.Fori(0, (B - 2) // 2) as i:
                batch(i * 2, 0)
                batch(i * 2 + 1, 1)

            def weights_low(piece):
                cols = slice(piece * WPIECE, (piece + 1) * WPIECE)
                pool.wait_ge(w_hi_set, piece + 1)
                nc.gpsimd.tensor_tensor(w_lo[:, cols], w_lo[:, cols], w_hi[:, cols].bitcast(F32),
                                        ALU.subtract).then_inc(w_lo_set, 1)

            def gate_low(c):
                for k in range(0, NK, 2):
                    pool.wait_ge(g_hi_act, c * (NK // 2) + k // 2 + 1)
                    tok = slice(c * CH, (c + 1) * CH)
                    nc.gpsimd.tensor_tensor(g_parts[:, 1, k, tok], act_f[:, GPLACE[c], k, :],
                                            g_parts[:, 0, k, tok].bitcast(F32), ALU.subtract).then_inc(g_lo_pool, 1)

            for piece in range(POOL_PIECES):
                weights_low(piece)
            inv_std((B - 2) * 2 + NCH + 1, TPB)
            inv_std((B - 2) * 2 + NCH + 2, TPB)
            gate_low(0)
            gate_low(1)
            gate_low(2)
            inv_std((B - 1) * 2 + NCH + 1, TPB)
            inv_std((B - 1) * 2 + NCH + 2, TPB)
            gate_low(3)
            with pool.Fori(0, NCH) as c:
                inv_std(c + NCH + 2 * B + 1, TPC)

        @block.vector
        def _(dve):
            nc.vector.memset(pv[:, :], 0.0).then_inc(psum_zeroed, 1)

            held = [0]

            def hold(semaphore, value):
                dve.wait_ge(semaphore, value)
                if not isinstance(value, int):
                    held[0] += 1
                    nc.vector.memset(pad[0:1, held[0] % PADS:held[0] % PADS + 1], 0.0)

            def moments(src, tiles, base, at=0):
                for t in range(tiles):
                    last = nc.vector.bn_stats(stats[:, t, :], src(t))
                last.then_inc(dve_order, 1)
                hold(dve_order, base + 1)
                for t in range(tiles):
                    last = nc.vector.bn_aggr(mv[:, at + t, :], stats[:, t, :])
                last.then_inc(dve_order, 1)
                dve.wait_ge(dve_order, base + 2)
                var = mv[:, at:at + tiles, 1]
                nc.vector.tensor_scalar(var, var, EPS, None, ALU.add).then_inc(var_set, 1)

            def normalize(dst, src, t, at=0):
                return nc.vector.tensor_scalar(dst, src, mv[:, at + t, 0:1], rstd[:, at + t:at + t + 1],
                                               ALU.subtract, ALU.mult)

            def x_moments(c):
                dve.wait_ge(x_in[c], 16)
                moments(lambda t: xs[:, c * TPC + t, :], TPC, c * 2, c * TPC)

            def x_normalize(c):
                dve.wait_ge(rstd_set, c + 1)
                if c >= 2:
                    dve.wait_ge(xnT_ready, c - 1)
                for t in range(TPC):
                    last = normalize(x_norm[c % 2][:, t, :], xs[:, c * TPC + t, :], t, c * TPC)
                last.then_inc(xn_set, 1)

            x_moments(0)
            x_moments(1)
            x_normalize(0)
            x_moments(2)
            x_normalize(1)
            dve.wait_ge(qkv_w_in, 112)
            nc.vector.tensor_scalar(bq_sb[:, 0:1], bq_sb[:, 0:1], scale, None, ALU.mult).then_inc(bq_scaled, 1)
            x_moments(3)
            nc.vector.tensor_copy(identr[:, :], ident[:, :]).then_inc(identr_set, 1)
            for c in range(NCH):
                if c + 2 < NCH:
                    x_normalize(c + 2)
                dve.wait_ge(v_ready, c + 1)
                dve.wait_ge(const_set, 2)
                nc.vector.tensor_tensor(
                    vx[:, c * TPC:(c + 1) * TPC, :, 0:DK],
                    bank[3].rearrange("p (t h d) -> p t h d", t=TPC, h=H),
                    bv_bc[:, :].rearrange("p (o h d) -> p o h d", o=1, h=H).broadcast_to((P, TPC, H, DK)),
                    ALU.add).then_inc(v_set, 1)
                for i in range(2):
                    dve.wait_ge(qk_hi_set, c * 2 + (i + 1))
                    nc.vector.tensor_tensor(qk_lo[c][:, i, :], qk_f[:, c % 2, i, :],
                                            qk_hi[c][:, i, :].bitcast(F32), ALU.subtract).then_inc(qk_lo_set, 1)
            def maxima(b, s, first=False):
                for it in range(TPB):
                    tile = ms_first[2 * (s % 2) + it] if first else ms[it]
                    hold(ms_ready, b * (2 * PAIRS) + (2 * s + it + 1))
                    for k in range(2):
                        h = 2 * s + k
                        col = P - it * P
                        last = nc.vector.tensor_tensor_reduce(
                            out=tile[:, k, :], in0=tile[:, k, :], in1=reverse(bias_max[:, h, WIN - S - col:WIN - col]), scale=1.0,
                            scalar=-3.4e38, op0=ALU.add, op1=ALU.max, accum_out=mx[:, it, h:h + 1])
                    last.then_inc(ms_read, 1)

            base = 2 * NCH

            def weigh(b, it):
                dve.wait_ge(o_ready, b * TPB + it + 1)
                heads = misc[:, :].rearrange("p (h c) -> p h c", h=H)
                n = b * 6 + base + 1 + it
                nc.vector.reciprocal(rsum[:, :], heads[:, :, DK]).then_inc(dve_order, 1)
                dve.wait_ge(dve_order, n)
                nc.vector.tensor_tensor(
                    on[:, it, :].rearrange("p (h d) -> p h d", h=H), heads[:, :, 0:DK],
                    rsum[:, :].rearrange("p (h o) -> p h o", o=1).broadcast_to((P, H, DK)),
                    ALU.mult).then_inc(on_set, 1)

            dve.wait_ge(out_w_in, 32)

            def attn_moments(b):
                dve.wait_ge(y_ready, b + 1)
                nc.vector.tensor_tensor(y[:, :, :], misc[:, 0:TPB * D].rearrange("p (t d) -> p t d", t=TPB),
                                        bo_bc[:, :].rearrange("p (o d) -> p o d", o=1).broadcast_to((P, TPB, D)),
                                        ALU.add).then_inc(y_read, 1)
                hold(y_read, b + 1)
                moments(lambda t: y[:, t, :], TPB, b * 6 + base + 2)

            def residual(b):
                dve.wait_ge(rstd_set, b * 2 + NCH + 1)
                for t in range(TPB):
                    last = normalize(y[:, t, :], y[:, t, :], t)
                last.then_inc(y_norm, 1)
                dve.wait_ge(y_norm, b + 1)
                xb = xs[:, bass.ds(b * TPB, TPB), :] if not isinstance(b, int) else xs[:, TPB * b:TPB * b + TPB, :]
                nc.vector.tensor_tensor(xb, xb, y[:, :, :], ALU.add).then_inc(x1_set, 1)
                hold(x1_set, b + 1)
                moments(lambda t: xs[:, bass.ds(b * TPB + t, 1), :].rearrange("p o d -> p (o d)"), TPB,
                        b * 6 + base + 4)

            def second_norm(b):
                dve.wait_ge(rstd_set, b * 2 + NCH + 2)
                if not (isinstance(b, int) and b == 0):
                    dve.wait_ge(zT_ready, b)
                for t in range(TPB):
                    last = normalize(z[:, t, :], xs[:, bass.ds(b * TPB + t, 1), :].rearrange("p o d -> p (o d)"), t)
                last.then_inc(z_set, 1)

            def z_low(b):
                dve.wait_ge(z_hi_set, b + 1)
                tok = bass.ds(b * S, S)
                nc.vector.tensor_tensor(z_parts[:, 1, tok], misc[:, 0:S], z_parts[:, 0, tok].bitcast(F32),
                                        ALU.subtract).then_inc(z_lo_set, 1)

            def weights_low(piece):
                cols = slice(piece * WPIECE, (piece + 1) * WPIECE)
                if piece < POOL_PIECES:
                    dve.wait_ge(w_lo_set, piece + 1)
                else:
                    dve.wait_ge(w_hi_set, piece + 1)
                    nc.vector.tensor_tensor(w_lo[:, cols], w_lo[:, cols], w_hi[:, cols].bitcast(F32),
                                            ALU.subtract).then_inc(w_lo_dve, 1)
                    dve.wait_ge(w_lo_dve, piece - POOL_PIECES + 1)
                nc.vector.tensor_reduce(w_low_max[:, piece:piece + 1], w_lo[:, cols], AX.X, ALU.max,
                                        apply_absolute_value=True).then_inc(w_low_max_set, 1)

            def add_bias(b, s):
                i = ADDED.index(s)
                tile = st[s % 2][:, :, :].rearrange("p k (j n) -> p k j n", j=2)
                view = bias_added[:, i, :, :]
                bias = bass.AP(tensor=view.tensor, offset=view.offset + WIN - 1,
                               ap=[list(view.ap[0]), [WIN, 2], [-P, 2], [-1, S]])
                dve.wait_ge(st_ready, b * PAIRS + (s + 1))
                nc.vector.tensor_tensor(tile, tile, bias, ALU.add).then_inc(added_set, 1)

            for s in range(PAIRS):
                dve.wait_ge(max_bias_in[s // (PAIRS // 2)], 16)
                maxima(0, s, first=True)
            dve.wait_ge(added_in, 16 * len(ADDED))

            def batch(b, par, post=True, more=True):
                for s in range(PAIRS):
                    if not more:
                        for piece in LOW_AT[s]:
                            weights_low(piece)
                    if post:
                        if s in (2, 3):
                            weigh(b - 1, s - 2)
                        if s == 5:
                            attn_moments(b - 1)
                        if s == 6:
                            residual(b - 1)
                    if more:
                        maxima(b + 1, s)
                    if s in ADDED:
                        add_bias(b, s)
                    if post and s == 6:
                        second_norm(b - 1)
                    if post and s == 7:
                        z_low(b - 1)

            batch(0, 0, post=False)
            with dve.Fori(0, (B - 2) // 2) as i:
                batch(i * 2 + 1, 1)
                batch(i * 2 + 2, 0)
            batch(B - 1, 1, more=False)
            dve.wait_ge(w_low_max_set, WPIECES)
            nc.vector.tensor_reduce(w_low_top[:, :], w_low_max[:, :], AX.X, ALU.max).then_inc(w_low_top_set, 1)
            dve.wait_ge(w_low_row, 1)
            nc.vector.tensor_reduce(w_low_any[:, :], bank[0][0:1, 0:P], AX.X, ALU.max).then_inc(w_low_any_set, 1)

            base3 = base + 6 * B

            def layer_low(c, i, tiles=range(NK)):
                for k in tiles:
                    dve.wait_ge((a1_hi_set, a2_hi_set)[i], c * NK + (k + 1))
                    hi, lo = layer_parts(c, i, k)
                    nc.vector.tensor_tensor(lo, act_f[:, i, k, :], hi.bitcast(F32),
                                            ALU.subtract).then_inc((a1_lo_set, a2_lo_set)[i], 1)

            dve.wait_ge(scales_in, 80)

            def gates(c):
                def split(k):
                    n = c * (NK // 2) + k // 2 + 1
                    tok = slice(c * CH, (c + 1) * CH)
                    tile = act_f[:, GPLACE[c], k, :]
                    dve.wait_ge(gate_set, c * NK + k + 1)
                    nc.vector.tensor_copy(g_parts[:, 0, k, tok], tile).then_inc(g_hi_dve, 1)
                    dve.wait_ge(g_hi_dve, n)
                    nc.vector.tensor_tensor(g_parts[:, 1, k, tok], tile, g_parts[:, 0, k, tok].bitcast(F32),
                                            ALU.subtract).then_inc(g_lo_dve, 1)

                for k in range(NK):
                    dve.wait_ge(silu_done, c * NK + (k + 1))
                    if c == 2:
                        dve.wait_ge((g_lo_pool, g_lo_dve)[k % 2], NK // 2 + k // 2 + 1)
                    if c == 3:
                        dve.wait_ge(a1_lo_set, NK + k + 1)
                    nc.vector.scalar_tensor_tensor(
                        out=act_f[:, GPLACE[c], k, :], in0=bank[GBANK[k % 2][1]], scalar=hs[:, 1, k:k + 1],
                        in1=gate[:, k % 2, :], op0=ALU.mult, op1=ALU.mult).then_inc(gate_set, 1)
                    if k == 2:
                        split(1)
                split(3)

            gates(0)
            weigh(B - 1, 0)
            gates(1)
            weigh(B - 1, 1)
            layer_low(0, 0)
            gates(2)
            attn_moments(B - 1)
            layer_low(0, 1, (0, 1))
            residual(B - 1)
            layer_low(0, 1, (2, 3))
            second_norm(B - 1)
            layer_low(1, 0)
            z_low(B - 1)
            layer_low(1, 1)
            gates(3)

            def last_norm(c):
                dve.wait_ge(y3_set, c + 1)
                moments(lambda t: xn[:, t, :], TPC, c * 2 + base3)
                dve.wait_ge(rstd_set, c + (NCH + 2 * B + 1))
                for t in range(TPC):
                    last = normalize(xn[:, t, :], xn[:, t, :], t)
                last.then_inc(y3_norm, 1)
                dve.wait_ge(y3_norm, c + 1)
                xc = xs[:, bass.ds(c * TPC, TPC), :]
                nc.vector.tensor_tensor(xc, xc, xn[:, :, :], ALU.add).then_inc(out_set, 1)

            last_norm(0)
            with dve.Fori(2, NCH) as c:
                layer_low(c, 0)
                layer_low(c, 1)
                last_norm(c - 1)
            last_norm(NCH - 1)

        @block.scalar
        def _(act):
            for dst, src in ((bq_sb[:, 0:1], bq), (bq_sb[:, 1:2], bk), (bv_bc, bv.broadcast_to((P, D)))):
                act.dma_start(dst[:, :], src).then_inc(qkv_w_in, 16)
            for dst, src in ((wo_sb, wo), (bo_bc, bo.broadcast_to((P, D)))):
                act.dma_start(dst[:, :], src).then_inc(out_w_in, 16)
            act.wait_ge(const_set, 1)
            nc.scalar.activation(table_loaded[:, :], mhalf[:, 0:1], ACT.Exp)
            act.wait_ge(qkv_w_in, 112)
            for g in range(2):
                load_table(act, g)

            def keep_xT(c):
                act.wait_ge(xnT_ready, c + 1)
                if c > 0:
                    act.wait_ge(v_ready, c)
                nc.scalar.copy(xT[:, :], bank[TBANK[c % 2]]).then_inc(xT_set, 1)

            def table_high(g):
                act.wait_ge(raw_in[g % 2], 16 * (g // 2 + 1))
                nc.scalar.copy(table[:, 0, 4 * g:4 * g + 4, :], reverse_rows(bias_raw[g][:, :, :])).then_inc(table_hi_set, 1)

            keep_xT(0)
            act.wait_ge(bq_scaled, 1)
            for c in range(NCH):
                if c >= 2:
                    act.wait_ge(qk_lo_set, (c - 1) * 2)
                for i, (ready, banks) in enumerate(((q_ready, QBANK), (k_ready, KBANK))):
                    act.wait_ge(ready, c + 1)
                    nc.scalar.activation(qk_f[:, c % 2, i, :], bank[banks[c % 2]], ACT.Identity,
                                         bias=bq_sb[:, i:i + 1], scale=scale if i == 0 else 1.0).then_inc(qk_f_set, 1)
                if c + 1 < NCH:
                    keep_xT(c + 1)
                for i in range(2):
                    act.wait_ge(qk_f_set, c * 2 + (i + 1))
                    nc.scalar.copy(qk_hi[c][:, i, :], qk_f[:, c % 2, i, :]).then_inc(qk_hi_set, 1)
                if c < 2:
                    table_high(c)
            def minus_max(b, half):
                act.wait_ge(mT_ready, b * 2 + 1 + half)
                if not (isinstance(b, int) and b == 0):
                    act.wait_ge(mrow_in[half], b * 16)
                nc.scalar.mul(mrow[:, half, :], misc[0:HALF, 0:S], -1.0).then_inc(mrow_set, 1)

            table_high(2)
            minus_max(0, 0)
            table_high(3)


            def probabilities(b, s, first=False):
                if s in ADDED:
                    act.wait_ge(added_set, b * len(ADDED) + (ADDED.index(s) + 1))
                else:
                    act.wait_ge(st_ready, b * PAIRS + (s + 1))
                if not (first and s < PRING):
                    act.wait_ge(pv_ready, b * GROUPS + ((s - PRING) // 2 + 1))
                nc.scalar.activation(probs[:, s % PRING, :, :, :].rearrange("p k j n -> p (k j n)"),
                                     st[s % 2][:, :, :].rearrange("p k n -> p (k n)"), ACT.Exp).then_inc(exp_done, 1)

            def keep_weighted(b, par, g):
                act.wait_ge(pv_ready, b * GROUPS + (g + 1))
                nc.scalar.copy(oT[:, par, g, :], pv[:, 0:S]).then_inc(oT_set, 1)

            def keep_onT(b):
                act.wait_ge(onT_ready, b + 1)
                nc.scalar.copy(onT[:, :], misc[:, 0:S]).then_inc(onT_set, 1)

            def keep_zT(b):
                act.wait_ge(zT_ready, b + 1)
                nc.scalar.copy(z_parts[:, 0, bass.ds(b * S, S)], misc[:, 0:S]).then_inc(z_hi_set, 1)

            def weights_high(piece):
                act.wait_ge(ffn_w_in[matrix_of(piece)], 16)
                cols = slice(piece * WPIECE, (piece + 1) * WPIECE)
                nc.scalar.copy(w_hi[:, cols], w_lo[:, cols]).then_inc(w_hi_set, 1)

            act.wait_ge(table_lo_set, GROUPS - 1)

            def batch(b, par, first=False, more=True):
                for s in range(PAIRS):
                    if s == 1:
                        minus_max(b, 1)
                    if s == 4 and not first:
                        keep_onT(b - 1)
                    if s == 6 and more:
                        minus_max(b + 1, 0)
                    if not more:
                        for piece in HIGH_AT[s]:
                            weights_high(piece)
                    if s == 7 and not first and more:
                        keep_zT(b - 1)
                    if s == 0 and not first:
                        keep_weighted(b - 1, 1 - par, GROUPS - 1)
                    probabilities(b, s, first)
                    if first and s == 2:
                        act.wait_ge(table_lo_set, GROUPS)
                    if s >= 2 and s % 2 == 0:
                        keep_weighted(b, par, s // 2 - 1)

            batch(0, 0, first=True)
            with act.Fori(0, (B - 2) // 2) as i:
                batch(i * 2 + 1, 1)
                batch(i * 2 + 2, 0)
            batch(B - 1, 1, more=False)
            keep_zT(B - 2)
            keep_weighted(B - 1, 1, GROUPS - 1)
            act.wait_ge(scales_in, 80)

            def gates(c):
                def high(k):
                    act.wait_ge(gate_set, c * NK + (k + 1))
                    nc.scalar.copy(g_parts[:, 0, k, c * CH:(c + 1) * CH], act_f[:, GPLACE[c], k, :]).then_inc(g_hi_act, 1)

                for k in range(NK):
                    act.wait_ge(up_ready, c * NK + (k + 1))
                    if c * NK + k >= 2:
                        act.wait_ge(gate_set, c * NK + (k - 1))
                    nc.scalar.activation(gate[:, k % 2, :], bank[GBANK[k % 2][0]], ACT.Silu,
                                         scale=hs[:, 0, k:k + 1]).then_inc(silu_done, 1)
                    if k % 2 == 1:
                        high(k - 1)

            def gates_split(n):
                act.wait_ge(g_lo_pool, n * NK // 2)
                act.wait_ge(g_lo_dve, n * NK // 2)

            def layer(c, i, first=False):
                ready, done, hi_set, lo_set = ((a1_ready, a1_set, a1_hi_set, a1_lo_set),
                                               (a2_ready, a2_set, a2_hi_set, a2_lo_set))[i]
                for k in range(NK):
                    act.wait_ge(ready, c * NK + (k + 1))
                    if not first:
                        act.wait_ge(lo_set, c * NK + (k - NK + 1))
                    nc.scalar.activation(act_f[:, i, k, :], bank[HBANK[i][k]], ACT.Gelu,
                                         scale=hs[:, 2 + i, k:k + 1]).then_inc(done, 1)
                    act.wait_ge(done, c * NK + (k + 1))
                    nc.scalar.copy(layer_parts(c, i, k)[0], act_f[:, i, k, :]).then_inc(hi_set, 1)

            def keep_y3T(c):
                act.wait_ge(y3_ready, c + 1)
                nc.scalar.mul(y3T[:, :], bank[7], w3s_sb[:, 0:1]).then_inc(y3T_set, 1)

            def keep_y3(c, first=False):
                act.wait_ge(y3_back, c + 1)
                if not first:
                    act.wait_ge(out_set, c)
                nc.scalar.copy(xn[:, :, :].rearrange("p t d -> p (t d)"), bank[7]).then_inc(y3_set, 1)

            gates(0)
            gates(1)
            gates_split(1)
            layer(0, 0, first=True)
            keep_onT(B - 1)
            gates(2)
            gates_split(3)
            layer(0, 1, first=True)
            layer(1, 0)
            keep_zT(B - 1)
            layer(1, 1)
            keep_y3T(0)
            gates(3)
            keep_y3(0, first=True)
            gates_split(NCH)
            with act.Fori(2, NCH) as c:
                layer(c, 0)
                keep_y3T(c - 1)
                layer(c, 1)
                keep_y3(c - 1)
            keep_y3T(NCH - 1)
            keep_y3(NCH - 1)

        @block.tensor
        def _(pe):
            mm = nc.tensor.matmul
            pe.wait_ge(qkv_w_in, 112)

            def x_T(c):
                pe.wait_ge(xn_set, c + 1)
                if c >= 2:
                    pe.wait_ge(xT_set, c - 1)
                for t in range(TPC):
                    last = nc.tensor.transpose(bank[TBANK[c % 2]][:, t * P:(t + 1) * P], x_norm[c % 2][:, t, :],
                                               ident[:, :])
                last.then_inc(xnT_ready, 1)

            x_T(0)
            for c in range(NCH):
                if c + 1 < NCH:
                    x_T(c + 1)
                pe.wait_ge(xT_set, c + 1)
                if c >= 2:
                    pe.wait_ge(qk_f_set, (c - 1) * 2)
                mm(bank[QBANK[c % 2]], wq_sb[:, :], xT[:, :], start=True, stop=True).then_inc(q_ready, 1)
                mm(bank[KBANK[c % 2]], wk_sb[:, :], xT[:, :], start=True, stop=True).then_inc(k_ready, 1)
                if c > 0:
                    pe.wait_ge(v_set, c)
                for t in range(TPC):
                    last = mm(bank[3][:, t * P:(t + 1) * P], xT[:, t * P:(t + 1) * P], wv_sb[:, :],
                              start=True, stop=True)
                last.then_inc(v_ready, 1)

            def rows(r, par, h, extra):
                r0 = 64 * (h // HALF)
                return r[r0:r0 + KROWS + extra, par, h % HALF, :]

            def max_scores(b, par, s, first=False):
                if s % (PAIRS // 2) == 0:
                    pe.wait_ge(rows_in[s // (PAIRS // 2)][par], b * (ROW_DMAS * 8) + ROW_DMAS * (16 - 8 * par))
                for it in range(TPB):
                    tile, n = ms[it], 2 * s + it
                    if first:
                        tile = ms_first[2 * (s % 2) + it]
                        if n >= 4:
                            pe.wait_ge(ms_read, n - 3)
                    else:
                        pe.wait_ge(ms_read, b * (2 * PAIRS) + (n - 1))
                    for k in range(2):
                        h = 2 * s + k
                        last = mm(tile[:, k, :], rows(q_rows, par, h, 0)[:, it * P:(it + 1) * P],
                                  rows(k_rows, par, h, 0), start=True, stop=True)
                    last.then_inc(ms_ready, 1)

            def maxima_T(b, half):
                pe.wait_ge(ms_read, b * (2 * PAIRS) + PAIRS * (half + 1))
                for it in range(TPB):
                    last = mm(misc[0:HALF, it * P:(it + 1) * P], mx[:, it, half * HALF:(half + 1) * HALF],
                              ident[:, :], start=True, stop=True)
                last.then_inc(mT_ready, 1)

            def scores(b, par, s, first=False):
                if s % (PAIRS // 2) == 0:
                    pe.wait_ge(mrow_in[s // (PAIRS // 2)], b * 16 + 16)
                if not (first and s < 2):
                    pe.wait_ge(exp_done, b * PAIRS + (s - 1))
                if first:
                    pe.wait_ge(table_lo_set, s // 2 + 1)
                added = s in ADDED
                if not added:
                    for k in range(2):
                        for a in range(2):
                            mm(st[s % 2][:, k, :], identr[:, :], windows(table[:, a, 2 * s + k, :], 0, P, 2, S),
                               start=(a == 0), stop=False)
                for k in range(2):
                    h = 2 * s + k
                    for j, jt in enumerate((1, 0)):
                        last = mm(st[s % 2][:, k, j * S:(j + 1) * S], rows(k_rows, par, h, 1)[:, jt * P:(jt + 1) * P],
                                  rows(q_rows, par, h, 1), start=added, stop=(added or j == 1))
                last.then_inc(st_ready, 1)

            def weighted(b, par, g, first=False):
                pe.wait_ge(exp_done, b * PAIRS + (2 * g + 2))
                if g == 0:
                    pe.wait_ge(v_near_set, b + 1)
                if not (first and g == 0):
                    pe.wait_ge(oT_set, b * GROUPS + g)
                for j, jt in enumerate((1, 0)):
                    for r in range(4):
                        h = 4 * g + r
                        last = mm(pv[32 * r:32 * r + VC, 0:S], v_near[:, par, jt, h, :],
                                  probs[:, (2 * g + r // 2) % PRING, r % 2, j, :], start=(j == 0), stop=(j == 1))
                last.then_inc(pv_ready, 1)

            def back(b, par, it):
                if it == 0:
                    pe.wait_ge(oT_set, b * GROUPS + GROUPS)
                else:
                    pe.wait_ge(on_set, b * TPB + it)
                for g in range(GROUPS):
                    last = nc.tensor.transpose(misc[:, g * P:(g + 1) * P], oT[:, par, g, it * P:(it + 1) * P],
                                               ident[:, :])
                last.then_inc(o_ready, 1)

            def heads_T(b):
                pe.wait_ge(on_set, b * TPB + TPB)
                for it in range(TPB):
                    last = nc.tensor.transpose(misc[:, it * P:(it + 1) * P], on[:, it, :], ident[:, :])
                last.then_inc(onT_ready, 1)

            def project(b):
                pe.wait_ge(onT_set, b + 1)
                for it in range(TPB):
                    last = mm(misc[:, it * P:(it + 1) * P], onT[:, it * P:(it + 1) * P], wo_sb[:, :],
                              start=True, stop=True)
                last.then_inc(y_ready, 1)

            def norm_T(b):
                pe.wait_ge(z_set, b + 1)
                for it in range(TPB):
                    last = nc.tensor.transpose(misc[:, it * P:(it + 1) * P], z[:, it, :], ident[:, :])
                last.then_inc(zT_ready, 1)

            pe.wait_ge(qk_f_set, 2 * NCH)
            pe.wait_ge(v_set, NCH)
            for s in range(PAIRS):
                if s == 6:
                    maxima_T(0, 0)
                max_scores(0, 0, s, first=True)
            pe.wait_ge(identr_set, 1)
            pe.wait_ge(ones_set, 2)
            pe.wait_ge(out_w_in, 32)
            pe.wait_ge(psum_zeroed, 1)
            pe.wait_ge(ms_read, 2 * PAIRS)

            def batch(b, par, first=False, more=True):
                for s in range(PAIRS):
                    if more:
                        max_scores(b + 1, 1 - par, s)
                    if s == 1:
                        if not more:
                            pe.wait_ge(z_lo_set, b - 1)
                        if first:
                            pe.wait_ge(mrow_set, 1)
                        else:
                            pe.wait_ge(oT_set, b * GROUPS)
                        maxima_T(b, 1)
                    if s == 7 and not first and more:
                        pe.wait_ge(mrow_set, b * 2 + 3)
                        norm_T(b - 1)
                    if s == 4 and not first:
                        project(b - 1)
                    scores(b, par, s, first)
                    if s == 0 and not first:
                        weighted(b - 1, 1 - par, GROUPS - 1)
                    if s >= 2 and s % 2 == 0:
                        weighted(b, par, s // 2 - 1, first)
                    if s == 1 and not first:
                        pe.wait_ge(mrow_set, b * 2 + 2)
                        back(b - 1, 1 - par, 0)
                    if s == 2 and not first:
                        back(b - 1, 1 - par, 1)
                    if s == 3 and not first:
                        heads_T(b - 1)
                    if s == 5 and more:
                        if first:
                            pe.wait_ge(mrow_set, 2)
                        else:
                            pe.wait_ge(y_read, b)
                        maxima_T(b + 1, 0)

            batch(0, 0, first=True)
            with pe.Fori(0, (B - 2) // 2) as i:
                batch(i * 2 + 1, 1)
                batch(i * 2 + 2, 0)
            batch(B - 1, 1, more=False)
            pe.wait_ge(y_read, B - 1)
            norm_T(B - 2)
            weighted(B - 1, 1, GROUPS - 1)
            pe.wait_ge(w_low_top_set, 1)
            pe.wait_ge(exp_done, B * PAIRS)
            mm(bank[0][0:1, 0:P], w_low_top[:, :], ident[:, :], start=True, stop=True).then_inc(w_low_row, 1)

            def product(o, weight, x, exact, first=True, last=True):
                hi, lo = x
                w = w_hi[:, weight]
                mm(o, w, hi, start=first, stop=False)
                done = mm(o, w, lo, start=False, stop=last and exact)
                if not exact:
                    mm(o, w_lo[:, weight], hi.bitcast(F32), start=False, stop=False)
                    done = mm(o, w_lo[:, weight], lo.bitcast(F32), start=False, stop=last)
                return done

            def columns(at, j, k, width):
                return slice(at + j * width + k * P, at + j * width + (k + 1) * P)

            def gates(c, exact):
                zc = [z_parts[:, a, c * CH:(c + 1) * CH] for a in range(2)]
                for k in range(NK):
                    if c * NK + k >= 2:
                        pe.wait_ge(gate_set, c * NK + k - 1)
                    product(bank[GBANK[k % 2][0]], columns(W1, 0, k, HID), zc, exact)
                    product(bank[GBANK[k % 2][1]], columns(W2, 0, k, HID), zc, exact).then_inc(up_ready, 1)

            def layer1(c, exact, first=False):
                pe.wait_ge(g_hi_act, c * (NK // 2) + NK // 2)
                pe.wait_ge(g_lo_pool, c * (NK // 2) + NK // 2)
                pe.wait_ge(g_lo_dve, c * (NK // 2) + NK // 2)
                for k in range(NK):
                    if k < 2 and not first:
                        pe.wait_ge(a2_set, c * NK + (k - 1))
                    if k == 3:
                        pe.wait_ge(a1_set, c * NK + 1)
                    for j in range(NK):
                        last = product(bank[HBANK[0][k]], columns(W_H1, j, k, HID), layer_parts(c, 1, j), exact,
                                       first=(j == 0), last=(j == NK - 1))
                    last.then_inc(a1_ready, 1)

            def layer2(c, exact):
                for k in range(NK):
                    if k < 3:
                        pe.wait_ge(a1_set, c * NK + (k + 2))
                    else:
                        pe.wait_ge(a2_set, c * NK + 1)
                    for j in range(NK):
                        if k == 0:
                            pe.wait_ge(a1_lo_set, c * NK + (j + 1))
                        last = product(bank[HBANK[1][k]], columns(W_H2, j, k, HID), layer_parts(c, 0, j), exact,
                                       first=(j == 0), last=(j == NK - 1))
                    last.then_inc(a2_ready, 1)

            def layer3(c, exact, first=False):
                if not first:
                    pe.wait_ge(y3_set, c)
                for j in range(NK):
                    pe.wait_ge(a2_lo_set, c * NK + (j + 1))
                    last = product(bank[7], columns(W3, j, 0, D), layer_parts(c, 1, j), exact,
                                       first=(j == 0), last=(j == NK - 1))
                last.then_inc(y3_ready, 1)

            def tokens_back(c):
                pe.wait_ge(y3T_set, c + 1)
                for t in range(TPC):
                    last = nc.tensor.transpose(bank[7][:, t * P:(t + 1) * P], y3T[:, t * P:(t + 1) * P], ident[:, :])
                last.then_inc(y3_back, 1)

            def ffn(exact):
                gates(0, exact)
                pe.wait_ge(z_lo_set, B - 1)
                back(B - 1, 1, 0)
                gates(1, exact)
                back(B - 1, 1, 1)
                layer1(0, exact, first=True)
                heads_T(B - 1)
                gates(2, exact)
                project(B - 1)
                layer2(0, exact)
                layer1(1, exact)
                pe.wait_ge(y_read, B)
                norm_T(B - 1)
                layer2(1, exact)
                pe.wait_ge(z_hi_set, B)
                pe.wait_ge(z_lo_set, B)
                layer3(0, exact, first=True)
                gates(3, exact)
                tokens_back(0)
                with pe.Fori(2, NCH) as c:
                    layer1(c, exact)
                    layer3(c - 1, exact)
                    layer2(c, exact)
                    tokens_back(c - 1)
                layer3(NCH - 1, exact)
                tokens_back(NCH - 1)

            pe.wait_ge(w_hi_set, WPIECES)
            pe.wait_ge(w_lo_set, POOL_PIECES)
            pe.wait_ge(w_lo_dve, WPIECES - POOL_PIECES)
            pe.wait_ge(w_low_any_set, 1)
            some_low = pe.value_load(w_low_any[0:1, 0:1].bitcast(I32))
            with pe.If(some_low != 0):
                ffn(exact=False)
            with pe.Else():
                ffn(exact=True)

    return nc


def kernel(**inputs):
    import numpy as np
    import concourse.bacc as bacc
    from concourse.bass_utils import run_bass_kernel_spmd

    a = {k.removeprefix("L0_"): np.asarray(v) for k, v in inputs.items()}
    w = a["attn_W_qkv"]
    bqkv = a["attn_b_qkv"]
    rel = np.ascontiguousarray(a["attn_rel_bias"].T)
    pad = ((0, 0), (P - 1, EXT - REL - (P - 1)))
    col = lambda v: v.reshape(-1, 1)
    by_dim = lambda m: m.reshape(-1, H, DK).transpose(0, 2, 1).reshape(-1, D)
    tiles = lambda v: v.reshape(NK, P).T
    weights = lambda m: m.T.reshape(NK, P, -1).transpose(1, 0, 2).reshape(P, -1)
    arrays = {
        "x": a["attn_x"].reshape(TOK, D),
        "wq": by_dim(w[:, 0:D]), "wk": by_dim(w[:, D:2 * D]), "wv": w[:, 2 * D:3 * D],
        "bq": by_dim(bqkv[None, 0:D]).T, "bk": by_dim(bqkv[None, D:2 * D]).T, "bv": bqkv[None, 2 * D:3 * D],
        "wo": a["attn_W_out"], "bo": a["attn_b_out"][None, :],
        "ext": np.pad(rel, pad, mode="edge")[:, ::-1], "ext_max": np.pad(rel[:, ::-1], pad, mode="edge")[:, ::-1],
        "w1": a["ffn_w1_w"].T, "s1": tiles(a["ffn_w1_s"]), "w2": a["ffn_w2_w"].T, "s2": tiles(a["ffn_w2_s"]),
        "h1": weights(a["ffn_h1_w"]), "h1s": tiles(a["ffn_h1_s"]),
        "h2": weights(a["ffn_h2_w"]), "h2s": tiles(a["ffn_h2_s"]),
        "w3": weights(a["ffn_w3_w"]), "w3s": col(a["ffn_w3_s"]),
        "ident_in": np.eye(P, dtype=np.float32),
    }
    arrays = {k: np.ascontiguousarray(v) for k, v in arrays.items()}
    nc = bacc.Bacc("TRN2", target_bir_lowering=False, num_devices=1)
    args = [nc.dram_tensor(k, v.shape, mybir.dt.from_np(v.dtype), kind="ExternalInput").ap() for k, v in arrays.items()]
    out = nc.dram_tensor("out", (TOK, D), F32, kind="ExternalOutput").ap()
    build(nc, *args, out)
    r = run_bass_kernel_spmd(nc, [arrays], core_ids=[0])
    return r.results[0]["out"].reshape(B, S, D)
```
